# Optimizing a Trainium2 kernel written in Bass

```python
import numpy as np
import jax
import jax.numpy as jnp

def _softmax(x, axis=-1):
    return jax.nn.softmax(x, axis=axis)
def _gelu(x):
    return jax.nn.gelu(x, approximate=True)
def _silu(x):
    return jax.nn.silu(x)
def _sigmoid(x):
    return jax.nn.sigmoid(x)
def _layernorm(x, axis=-1, eps=1e-5):
    m = jnp.mean(x, axis=axis, keepdims=True)
    v = jnp.var(x, axis=axis, keepdims=True)
    return (x - m) / jnp.sqrt(v + eps)
def _scatter_add(tgt, idx, src, axis=0):
    return tgt.at[idx].add(src)
def _segment_sum(src, seg, n):
    return jax.ops.segment_sum(src, seg, n)

kernel_name = 'mk_conv_preact_d2_conv_nchw128_485cb5'

def setup_inputs(seed: int = 0):
    np.random.seed(seed)
    _w = jnp.asarray
    def _rec_inputs():
        import jax
        import jax.numpy as jnp
        _gk = jax.random.key(seed)
        x = -0.000125 + 0.9999 * jax.random.normal(jax.random.fold_in(_gk, 1), (16, 128, 128, 128), jnp.float32)
        return x
    x = _rec_inputs()
    def _L0_conv_setup():
        import jax, jax.numpy as jnp
        import numpy as np
        B, DIM, H, W = (16, 128, 128, 128)
        HID = 2 * DIM
        K = 3

        def _conv1x1(x, w, b):
            return jnp.einsum('bchw,oc->bohw', x, w) + b[None, :, None, None]
        key = jax.random.key(seed)
        ks = jax.random.split(key, 10)
        s = 0.05
        return {'x': jax.random.normal(ks[0], (B, DIM, H, W), dtype=jnp.float32), 'w_in': jax.random.normal(ks[1], (HID, DIM), dtype=jnp.float32) * s, 'b_in': jax.random.normal(ks[2], (HID,), dtype=jnp.float32) * s, 'kg_w1': jax.random.normal(ks[3], (HID, HID), dtype=jnp.float32) * s, 'kg_b1': jax.random.normal(ks[4], (HID,), dtype=jnp.float32) * s, 'kg_w2': jax.random.normal(ks[5], (HID * K * K, HID), dtype=jnp.float32) * s, 'kg_b2': jax.random.normal(ks[6], (HID * K * K,), dtype=jnp.float32) * s, 'w_out': jax.random.normal(ks[7], (DIM, HID), dtype=jnp.float32) * s, 'b_out': jax.random.normal(ks[8], (DIM,), dtype=jnp.float32) * s}
    _L0_conv_all = _L0_conv_setup()
    _L0_conv_in = {k: v for k, v in _L0_conv_all.items() if k in ('w_in', 'b_in', 'kg_w1', 'kg_b1', 'kg_w2', 'kg_b2', 'w_out', 'b_out', )}
    del _L0_conv_all

    def _L1_conv_setup():
        import jax, jax.numpy as jnp
        import numpy as np
        B, C, H, W = (4, 128, 256, 256)
        key = jax.random.key(seed)
        k = jax.random.split(key, 6)
        x = jax.random.normal(k[0], (B, C, H, W), dtype=jnp.float32)
        freq_mask = jax.random.uniform(k[1], (1, C, 1, 1), dtype=jnp.float32)
        amp_w = jax.random.normal(k[2], (C, C), dtype=jnp.float32) * 0.05
        amp_b = jax.random.normal(k[3], (C,), dtype=jnp.float32) * 0.05
        phase_w = jax.random.normal(k[4], (C, C), dtype=jnp.float32) * 0.05
        phase_b = jax.random.normal(k[5], (C,), dtype=jnp.float32) * 0.05
        return {'x': x, 'freq_mask': freq_mask, 'amp_w': amp_w, 'amp_b': amp_b, 'phase_w': phase_w, 'phase_b': phase_b}
    _L1_conv_all = _L1_conv_setup()
    _L1_conv_in = {k: v for k, v in _L1_conv_all.items() if k in ('freq_mask', 'amp_w', 'amp_b', 'phase_w', 'phase_b', )}
    del _L1_conv_all

    return {
        "x": x,
        "L0_conv_w_in": _L0_conv_in["w_in"],
        "L0_conv_b_in": _L0_conv_in["b_in"],
        "L0_conv_kg_w1": _L0_conv_in["kg_w1"],
        "L0_conv_kg_b1": _L0_conv_in["kg_b1"],
        "L0_conv_kg_w2": _L0_conv_in["kg_w2"],
        "L0_conv_kg_b2": _L0_conv_in["kg_b2"],
        "L0_conv_w_out": _L0_conv_in["w_out"],
        "L0_conv_b_out": _L0_conv_in["b_out"],
        "L1_conv_freq_mask": _L1_conv_in["freq_mask"],
        "L1_conv_amp_w": _L1_conv_in["amp_w"],
        "L1_conv_amp_b": _L1_conv_in["amp_b"],
        "L1_conv_phase_w": _L1_conv_in["phase_w"],
        "L1_conv_phase_b": _L1_conv_in["phase_b"],
    }

def reference(x, L0_conv_w_in, L0_conv_b_in, L0_conv_kg_w1, L0_conv_kg_b1, L0_conv_kg_w2, L0_conv_kg_b2, L0_conv_w_out, L0_conv_b_out, L1_conv_freq_mask, L1_conv_amp_w, L1_conv_amp_b, L1_conv_phase_w, L1_conv_phase_b):
    import jax
    import jax.numpy as jnp
    def _L0_conv_ref(x, w_in, b_in, kg_w1, kg_b1, kg_w2, kg_b2, w_out, b_out):
        import jax, jax.numpy as jnp
        import numpy as np
        B, DIM, H, W = (16, 128, 128, 128)
        HID = 2 * DIM
        K = 3

        def _conv1x1(x, w, b):
            return jnp.einsum('bchw,oc->bohw', x, w) + b[None, :, None, None]
        b, _, h, w = x.shape
        xh = _conv1x1(x, w_in, b_in)
        c = xh.shape[1]
        pooled = jnp.mean(xh, axis=(2, 3))
        hcx = jax.nn.relu(pooled @ kg_w1.T + kg_b1)
        kernels = (hcx @ kg_w2.T + kg_b2).reshape(b, c, K, K)
        x_r = xh.reshape(1, b * c, h, w)
        k_r = kernels.reshape(b * c, 1, K, K)
        y = jax.lax.conv_general_dilated(x_r, k_r, window_strides=(1, 1), padding=((1, 1), (1, 1)), feature_group_count=b * c, dimension_numbers=('NCHW', 'OIHW', 'NCHW'))
        y = y.reshape(b, c, h, w)
        y = y * jnp.tanh(jax.nn.softplus(y))
        return _conv1x1(y, w_out, b_out)

    def _L1_conv_ref(x, freq_mask, amp_w, amp_b, phase_w, phase_b):
        import jax, jax.numpy as jnp
        import numpy as np
        B, C, H, W = (4, 128, 256, 256)
        xf = jnp.fft.fftshift(jnp.fft.fft(x, axis=1), axes=1) * freq_mask
        amp = jnp.einsum('bchw,oc->bohw', xf.real, amp_w) + amp_b[None, :, None, None]
        ph = jnp.einsum('bchw,oc->bohw', xf.imag, phase_w) + phase_b[None, :, None, None]
        xc = jax.lax.complex(amp, ph)
        xi = jnp.fft.ifft(jnp.fft.ifftshift(xc, axes=1), axis=1)
        return jax.nn.relu(jnp.real(xi))

    def _gn(v, G=32, eps=1e-5):
        B_, C_, H_, W_ = v.shape
        g = v.reshape(B_, G, C_ // G, H_, W_)
        m = jnp.mean(g, axis=(2, 3, 4), keepdims=True)
        s = jnp.var(g, axis=(2, 3, 4), keepdims=True)
        return ((g - m) / jnp.sqrt(s + eps)).reshape(v.shape)

    def _ln_c(v, eps=1e-6):
        m = jnp.mean(v, axis=1, keepdims=True)
        s = jnp.var(v, axis=1, keepdims=True)
        return (v - m) / jnp.sqrt(s + eps)

    def _ln_t(v, eps=1e-5):
        m = jnp.mean(v, axis=-1, keepdims=True)
        s = jnp.var(v, axis=-1, keepdims=True)
        return (v - m) / jnp.sqrt(s + eps)

    def _to_tokens(v):
        B_, C_, H_, W_ = v.shape
        return v.reshape(B_, C_, H_ * W_).transpose(0, 2, 1)
    def _from_tokens(t, like):
        B_, C_, H_, W_ = like.shape
        return t.transpose(0, 2, 1).reshape(B_, C_, H_, W_)

    x = x + _L0_conv_ref(_gn(x), L0_conv_w_in, L0_conv_b_in, L0_conv_kg_w1, L0_conv_kg_b1, L0_conv_kg_w2, L0_conv_kg_b2, L0_conv_w_out, L0_conv_b_out)
    x = x + _L1_conv_ref(_gn(x), L1_conv_freq_mask, L1_conv_amp_w, L1_conv_amp_b, L1_conv_phase_w, L1_conv_phase_b)
    return x


_drawn_inputs = setup_inputs


def setup_inputs(seed=0):
    import zlib

    import numpy as np

    out = dict(_drawn_inputs(seed))
    spreads = {}
    factors = {'L0_conv_b_in': 3.519,
     'L0_conv_kg_w1': 3.404,
     'L0_conv_kg_b1': 2.901,
     'L1_conv_amp_b': 26.813,
     'L1_conv_phase_b': 24.029}
    for name, (base, spread) in spreads.items():
        noise = np.random.default_rng([zlib.crc32(name.encode()), seed]).standard_normal(out[name].shape)
        drawn = base * np.exp(spread * noise) if base else spread * noise
        out[name] = jnp.asarray(drawn.astype(out[name].dtype))
    for name, factor in factors.items():
        out[name] = (out[name] * factor).astype(out[name].dtype)
    return out
```

```python
import concourse.bass as bass
from concourse import mybir
from contextlib import ExitStack

F32 = mybir.dt.float32
F16 = mybir.dt.float16
ALU = mybir.AluOpType
ACT = mybir.ActivationFunctionType

B, C, H, W = 16, 128, 128, 128
HID = 2 * C
TAPS = 9
ROWS = 8
SP = ROWS * W
TP = SP // 2
STRIPS = H // ROWS
QUADS = STRIPS // 4
PW = W + 2
RING = 32
XG = 6
AHEAD = 4
STAT = 20
LOADED = STAT + 1
GROUP = 4
EPS = 1e-5
EMAX = float(2 ** 30)


def conv_preact_kernel(nc, x, w_in_t, b_in, w1_t, b1, w2_t, b2, w_out_t, b_out, mask, amp_w, amp_b,
                       ph_w, ph_b, cos_m, sin_m, group_m, ident_m, valid_m, out):
    ctx = ExitStack()
    with ctx:
        def sb(name, shape, dt=F32):
            return ctx.enter_context(nc.sbuf_tensor(name, shape, dt))

        def pb(name, shape):
            return ctx.enter_context(nc.psum_tensor(name, shape, F32))

        def sem(name):
            return ctx.enter_context(nc.semaphore(name))

        vectors = sb("vectors", [C, 144])
        taken = [0]

        def few(n):
            taken[0] += n
            return vectors[:, taken[0] - n:taken[0]]

        X = sb("X", [C, XG * 4 * SP])
        XS = sb("XS", [C, 4, TP])
        hi = sb("hi", [C, RING + 2, PW], F16)
        lo = sb("lo", [C, RING + 2, PW], F16)
        xh = sb("xh", [C, RING + 2, PW])
        acc = sb("acc", [C, 2, SP])
        em = sb("em", [C, 2 * SP])
        wm = sb("wm", [C, 2 * SP])
        zt = sb("zt", [C, 2, TP])
        w2p = sb("w2p", [C, 2, 2, TAPS, HID], F16)
        w1t = sb("w1t", [C, 2, HID])
        wint = sb("wint", [C, HID])
        wn = sb("wn", [C, HID])
        woutt = sb("woutt", [C, 2, C])
        ident = sb("ident", [C, C])
        groupm = sb("groupm", [C, C])
        lt = sb("lt", [C, C])
        lpt = sb("lpt", [C, C])
        valid = sb("valid", [64, 6, W], F16)
        wst = sb("wst", [C, 2, TAPS * C], F16)
        wa = sb("wa", [C, 2, TAPS * C], F16)
        wtmp = sb("wtmp", [C, 3 * C])
        wb = sb("wb", [C, 2, C], F16)
        vbst = sb("vbst", [64, C], F16)
        vb = sb("vb", [64, C], F16)
        bx = sb("bx", [C, 64])
        bh = sb("bh", [C, TAPS], F16)
        hv = sb("hv", [C, 2, 4], F16)
        bk = few(TAPS)
        zrow = sb("zrow", [C, PW], F16)
        binp = few(2)
        b1p = few(2)
        b2p = few(2 * TAPS)
        boutp = few(1)
        spare = few(4)
        cl = few(1)
        lb = few(1)
        bpl = few(1)
        bnx = sb("bnx", [C, 2 * STRIPS, 6])
        bn1 = sb("bn1", [C, 2 * STRIPS, 6])
        kk = few(2 * TAPS)
        kb = few(TAPS)
        pooled = few(2)
        bp = few(2)
        pm = few(4)
        hcx = few(2)
        kraw = few(4 * TAPS)
        st = {}
        for who in ("x", "1"):
            st[who] = {k: few(n) for k, n in
                       (("agg", 2), ("gm", 2), ("t", 1), ("v", 1), ("ln", 1), ("r0", 1), ("r", 1), ("mm", 2))}

        w2t = X[:, STRIPS * SP:STRIPS * SP + 2 * TAPS * HID].rearrange("p (k t o) -> p k t o", k=2, t=TAPS)
        cosm, sinm, ampw, phw = (em[:, i * C:(i + 1) * C] for i in range(4))
        m1 = em[:, 4 * C:6 * C]
        small = em[:, 6 * C:6 * C + 4]
        maskp, ampb, phb, nphb = (small[:, i:i + 1] for i in range(4))

        psA = pb("psA", [C, 2, SP])
        psB = pb("psB", [C, TP])
        psO = pb("psO", [C, TP])
        psL = pb("psL", [C, TP])
        psM = pb("psM", [C, TP])

        s_const = sem("s_const")
        s_xin = [sem(f"s_xin{j}") for j in range(4)]
        s_first = [sem(f"s_first{n}") for n in range(STRIPS)]
        s_sin = [sem(f"s_sin{j}") for j in range(4)]
        s_out = [sem(f"s_out{j}") for j in range(4)]
        s_zero = sem("s_zero")
        s_hi = sem("s_hi")
        s_lo = sem("s_lo")
        s_xm = sem("s_xm")
        s_xe = sem("s_xe")
        s_cv = sem("s_cv")
        s_tap = sem("s_tap")
        s_exp = sem("s_exp")
        s_cl = sem("s_cl")
        s_act = sem("s_act")
        s_w = sem("s_w")
        s_om = sem("s_om")
        s_x1 = sem("s_x1")
        s_lm = sem("s_lm")
        s_re = sem("s_re")
        s_add = sem("s_add")
        s_bx = sem("s_bx")
        s_b1 = sem("s_b1")
        hk = {}
        for who in ("x", "1"):
            for k in ("agg", "mom", "gps", "gsb", "var", "ln", "r0", "r", "pool"):
                hk[who + k] = sem(f"s_{who}_{k}")
        s_wn = sem("s_wn")
        s_pps = sem("s_pps")
        s_psb = sem("s_psb")
        s_pl = sem("s_pl")
        s_hps = sem("s_hps")
        s_hcx = sem("s_hcx")
        s_hvh = sem("s_hvh")
        s_hvl = sem("s_hvl")
        s_ks = sem("s_ks")
        s_w2 = sem("s_w2")
        s_kps = sem("s_kps")
        s_ksb = sem("s_ksb")
        s_kk = sem("s_kk")
        s_bxr = sem("s_bxr")
        s_bst = sem("s_bst")
        s_tps = sem("s_tps")
        s_vst = sem("s_vst")
        s_kbc = sem("s_kbc")
        s_wt = sem("s_wt")
        s_wsh = sem("s_wsh")
        s_wsl = sem("s_wsl")
        s_wa = sem("s_wa")
        s_vb = sem("s_vb")
        s_kb = sem("s_kb")
        s_wbh = sem("s_wbh")
        s_wbl = sem("s_wbl")
        s_bpl = sem("s_bpl")
        s_lps = sem("s_lps")
        s_lpt = sem("s_lpt")
        s_lb = sem("s_lb")
        s_i = sem("s_i")
        s_j = sem("s_j")
        s_chain = {who: sem(f"s_chain_{who}") for who in ("x", "1")}

        s_apart = sem("s_apart")

        consts = [
            (cosm, cos_m), (sinm, sin_m), (ampw, amp_w), (phw, ph_w), (maskp, mask), (ampb, amp_b),
            (phb, ph_b), (groupm[:], group_m), (ident[:], ident_m), (valid[:], valid_m), (wint[:], w_in_t),
            (binp[:], b_in), (b1p[:], b1), (b2p[:], b2), (boutp[:], b_out), (w1t[:], w1_t),
            (woutt[:], w_out_t), (w2t, w2_t),
        ]

        block = ctx.enter_context(nc.Block())

        FREE = 2

        def snap(eng, v):
            return v if isinstance(v, int) else eng.snap(v)

        def apart(eng):
            eng.sem_inc(s_apart, 1)

        def last_bank(s, t):
            return psA[:, s % 2, t * TP:(t + 1) * TP]

        def slot(Q, k):
            return ((Q + (k % XG)) % XG) * (4 * SP)

        def image_loop(eng, prologue, quad, epilogue):
            prologue()
            for first in (True, False):
                def image(b):
                    quad(b, 0, b * QUADS, first, "head")
                    with eng.Fori(1, QUADS - 1) as q:
                        quad(b, q, b * QUADS + q, first, "mid")
                    quad(b, QUADS - 1, b * QUADS + QUADS - 1, first, "tail")
                if first:
                    image(0)
                else:
                    with eng.Fori(1, B) as b:
                        image(b)
            epilogue()

        def l1_strips(j, kind):
            if kind == "head" and j < 3:
                return []
            if kind == "tail" and j == 1:
                return [(-5, 2), (-5, 3)]
            if kind == "tail" and j >= 2:
                return [(-4, 2 * j - 4), (-4, 2 * j - 3)]
            return [(-5, j + 1)] if j < 3 else [(-4, 0)]

        @block.sync
        def _(eng):
            xr = x.rearrange("b c n -> c b n")
            outr = out.rearrange("b c n -> c b n")

            def load_x(n4, j, b, px, base, free, used):
                if free is not None:
                    eng.wait_ge(s_out[j], free)
                    apart(eng)
                if used is not None:
                    eng.wait_ge(s_hi, used)
                apart(eng)
                eng.dma_start(X[:, bass.ds(base + j * SP, SP)], xr[:, bass.ds(b, 1), bass.ds(px, SP)]
                              .rearrange("c b n -> c (b n)")).then_inc(s_xin[j], 16)

            def load_stat(i, b, px, used):
                if used is not None:
                    eng.wait_ge(s_bx, used)
                apart(eng)
                eng.dma_start(XS[:, i, :], xr[:, bass.ds(b, 1), bass.ds(px, TP)]
                              .rearrange("c b n -> c (b n)")).then_inc(s_sin[i], 16)

            def store(k, j, b, px, base, n):
                eng.wait_ge(s_add, 2 * n + 2 + FREE)
                eng.wait_ge(s_out[j], 16 * (k + 1))
                apart(eng)
                eng.dma_start(outr[:, bass.ds(b, 1), bass.ds(px, SP)].rearrange("c b n -> c (b n)"),
                              X[:, bass.ds(base + j * SP, SP)]).then_inc(s_out[j], 16)

            def constants():
                for j in range(4):
                    eng.dma_start(spare[:, j:j + 1], b_out).then_inc(s_out[j], 16)
                for dst, src in consts:
                    eng.dma_start(dst, src).then_inc(s_const, 16)

            def prologue():
                for n in range(STRIPS):
                    eng.dma_start(X[:, n * SP:(n + 1) * SP], xr[:, 0, n * SP:(n + 1) * SP]).then_inc(s_first[n], 16)
                    if n == 1:
                        constants()
                for c in range(2 * STRIPS, 2 * LOADED):
                    n = c // 2
                    load_stat(c % 4, n // STRIPS, (n % STRIPS) * SP + (c % 2) * TP,
                              c - 3 if c >= 2 * STRIPS + 4 else None)

            def quad(b, q, Q, first, kind):
                g0 = snap(eng, Q * 4)
                nxt = snap(eng, slot(Q, 1))
                old = snap(eng, slot(Q, -4))
                bl = snap(eng, (b + (1 if kind == "tail" else 0)) % B)
                ql = 0 if kind == "tail" else q + 1
                for j in range(4):
                    ns = snap(eng, g0 + j + LOADED)
                    for t in range(2):
                        i = (2 * (j + LOADED) + t) % 4
                        load_stat(i, (ns // STRIPS) % B, (ns % STRIPS) * SP + t * TP, 2 * ns + t - 3)
                    if not first:
                        for off, k in l1_strips(j, kind):
                            base = nxt if off == -5 else old
                            qq = q + off + QUADS
                            store(Q + off, k, b - 1, (qq * 4 + k) * SP, base, (Q + off) * 4 + k)
                    if not (first and kind != "tail"):
                        load_x(Q + 1, j, bl, (ql * 4 + j) * SP, nxt, None if first else 16 * (Q - 3), g0 + j + 1)

            def epilogue():
                Q = B * QUADS
                for s in range(STRIPS):
                    n = Q * 4 - STRIPS + s
                    store(Q - QUADS + s // 4, s % 4, B - 1, s * SP, slot(Q - QUADS + s // 4, 0), n)
                for j in range(4):
                    eng.wait_ge(s_out[j], 16 * (B * QUADS + 1))

            image_loop(eng, prologue, quad, epilogue)
            for j in range(4):
                eng.wait_ge(s_xin[j], 16 * (B * QUADS + 1 - QUADS))
                eng.wait_ge(s_sin[j], 16 * ((2 * (B * STRIPS + LOADED - STRIPS) + 3 - j) // 4))

        @block.scalar
        def _(eng):
            act = nc.scalar.activation

            def stats_group(who, i):
                eng.wait_ge(hk[who + "gps"], i + 1)
                act(st[who]["gm"][:], psM[:, 0:2], ACT.Copy).then_inc(hk[who + "gsb"], 1)

            def stats_rstd(who, i):
                d = st[who]
                eng.wait_ge(hk[who + "var"], i + 1)
                act(d["ln"][:], d["v"][:], ACT.Ln).then_inc(hk[who + "ln"], 1)
                eng.wait_ge(hk[who + "ln"], i + 1)
                act(d["r0"][:], d["ln"][:], ACT.Exp, scale=-0.5).then_inc(hk[who + "r0"], 1)

            def pooled_out(i):
                eng.wait_ge(s_pps, i + 1)
                act(pm[:], psM[:, 0:4], ACT.Copy).then_inc(s_psb, 1)

            def hidden_out(i):
                eng.wait_ge(s_hps, i + 1)
                for h in range(2):
                    last = act(hcx[:, h:h + 1], psM[:, h:h + 1], ACT.Relu, bias=b1p[:, h:h + 1])
                last.then_inc(s_hcx, 1)
                eng.wait_ge(s_hcx, i + 1)
                act(hv[:, :, 1], hcx[:], ACT.Copy).then_inc(s_hvh, 1)

            def kernels_out(i):
                eng.wait_ge(s_kps, i + 1)
                act(kraw[:], psM[:, 0:4 * TAPS], ACT.Copy).then_inc(s_ksb, 1)

            def bias_out(i):
                eng.wait_ge(s_tps, i + 1)
                act(vbst[:], psM[0:64, 0:C], ACT.Copy).then_inc(s_vst, 1)

            def taps_high(i, u):
                eng.wait_ge(s_wt, 3 * i + u + 1)
                act(wst[:, 0, 3 * u * C:3 * (u + 1) * C], wtmp[:], ACT.Copy).then_inc(s_wsh, 1)

            def switch_b(i, done):
                if done is not None:
                    eng.wait_ge(s_xm, done)
                eng.wait_ge(s_wn, i + 1)
                act(wb[:, 0, :], wn[:, C:HID], ACT.Copy).then_inc(s_wbh, 1)
                if done is not None:
                    eng.wait_ge(s_xe, done)
                eng.wait_ge(s_pl, i + 1)
                act(bpl[:], bp[:, 1:2], ACT.Copy).then_inc(s_bpl, 1)

            def switch_a(i, done):
                if done is not None:
                    eng.wait_ge(s_cv, done)
                eng.wait_ge(s_vst, i + 1)
                act(vb[:], vbst[:], ACT.Copy).then_inc(s_vb, 1)

            def cast(n, n4, j, base, row, there):
                if not there:
                    eng.wait_ge(s_xin[j], 16 * (n4 + 1 - QUADS))
                if not isinstance(n, int) or n >= 3:
                    eng.wait_ge(s_cv, n - 2)
                xs = X[:, bass.ds(base + j * SP, SP)].rearrange("p (r c) -> p r c", c=W)
                edge_row(eng, hi, j, row, lambda r: xs[:, r * (ROWS - 1), :])
                act(hi[:, 8 * j + 1:8 * j + 9, 1:1 + W], xs, ACT.Copy).then_inc(s_hi, 1)

            def edge_row(eng, ring, j, row, src, bias=None):
                if row == "top":
                    act(ring[:, 0, :], zrow[:], ACT.Copy)
                elif row == "bottom":
                    act(ring[:, RING + 1, :], zrow[:], ACT.Copy)
                elif j == 0 or j == 3:
                    dst = ring[:, RING + 1 if j == 0 else 0, 1:1 + W]
                    r = 0 if j == 0 else 1
                    if bias is None:
                        act(dst, src(r), ACT.Copy)
                    else:
                        act(dst, src(r), ACT.Identity, bias=bias)

            def evacuate(n, j, t, row, i):
                eng.wait_ge(s_xm, 2 * n + t + 1)
                if t == 0:
                    if not isinstance(n, int) or n >= 3:
                        eng.wait_ge(s_tap, (n - 2) * TAPS)
                    if row == "top":
                        eng.wait_ge(s_bpl, i + 1)
                ps = psB[:].rearrange("p (r c) -> p r c", c=W)
                if (j == 0 and t == 0) or (j == 3 and t == 1):
                    edge_row(eng, xh, j, row, lambda r: ps[:, r * 3, :], bias=bpl[:, 0:1])
                r0 = 8 * j + 4 * t + 1
                act(xh[:, r0:r0 + 4, 1:1 + W], ps, ACT.Identity, bias=bpl[:, 0:1]).then_inc(s_xe, 1)

            def mish_exp(n, par):
                if not isinstance(n, int) or n >= 1:
                    eng.wait_ge(s_w, n)
                eng.wait_ge(s_cv, n + 1)
                act(em[:, 0:SP], psA[:, par, :], ACT.Exp)
                eng.wait_ge(s_tap, (n + 1) * TAPS)
                act(em[:, SP:2 * SP], acc[:, par, :], ACT.Exp).then_inc(s_exp, 1)

            def mish_rest(n):
                eng.wait_ge(s_cl, n + 1)
                act(em[:], em[:], ACT.Square, bias=1.0).then_inc(s_act, 1)
                eng.wait_ge(s_act, 3 * n + 1)
                act(em[:], em[:], ACT.Ln, bias=1.0).then_inc(s_act, 1)
                eng.wait_ge(s_act, 3 * n + 2)
                act(em[:], em[:], ACT.Exp, scale=-1.0).then_inc(s_act, 1)

            def relu(n, t, i, ps=None):
                if i is not None:
                    eng.wait_ge(s_lb, i)
                eng.wait_ge(s_lm, 2 * n + t + 1)
                eng.wait_ge(s_add, 2 * n + t - 1 + FREE)
                act(zt[:, t, :], psL[:] if ps is None else ps, ACT.Relu, bias=lb[:, 0:1]).then_inc(s_re, 1)

            def layer1_bias(i):
                eng.wait_ge(s_lps, i + 1)
                eng.wait_ge(s_re, 2 * STRIPS * i + FREE)
                act(lb[:], psM[:, 0:1], ACT.Identity, bias=cl[:, 0:1], scale=-1.0).then_inc(s_lb, 1)

            def prologue():
                nc.scalar.preload_act_table_set("natural_log_exp_and_others")
                eng.wait_ge(s_const, 16 * len(consts))
                eng.wait_ge(s_i, 1)
                act(m1[:, 0:C], psM[:, 0:C], ACT.Copy, scale=maskp)
                act(m1[:, C:2 * C], psM[:, C:2 * C], ACT.Copy, scale=maskp)
                act(nphb, phb, ACT.Copy, scale=-1.0).then_inc(s_j, 1)
                eng.wait_ge(s_i, 2)
                act(lt[:], psM[:, 0:C], ACT.Copy, scale=1.0 / C)
                act(cl[:], psM[:, C:C + 1], ACT.Copy, scale=1.0 / C)
                act(woutt[:], woutt[:], ACT.Copy, scale=-2.0).then_inc(s_j, 1)
                eng.wait_ge(s_j, 2)
                eng.wait_ge(s_zero, 6)
                for t in range(FREE):
                    act(zt[:, t, 0:PW], zrow[:], ACT.Copy).then_inc(s_re, 1)
                act(w2p[:, 0], w2t, ACT.Copy).then_inc(s_w2, 1)
                stats_group("x", 0)
                stats_rstd("x", 0)
                pooled_out(0)
                switch_b(0, None)
                hidden_out(0)
                kernels_out(0)
                bias_out(0)
                for u in range(3):
                    taps_high(0, u)
                eng.wait_ge(s_zero, 6)
                for n in range(2):
                    cast(n, 0, n, 0, "top" if n == 0 else None, True)
                for n in range(2):
                    for t in range(2):
                        evacuate(n, n, t, "top" if n == 0 else None, 0)

            def quad(b, q, Q, first, kind):
                g0 = snap(eng, Q * 4)
                cur = snap(eng, slot(Q, 0))
                nxt = snap(eng, slot(Q, 1))
                for j in range(4):
                    head, tail = kind == "head", kind == "tail"
                    if head and j == 0:
                        switch_a(b, None if first else g0)
                    if tail and j == 2:
                        switch_b(b + 1, 2 * (g0 + 4))
                    j2 = (j + 2) % 4
                    n2 = g0 + j + 2
                    row = "bottom" if tail and j == 1 else "top" if tail and j == 2 else None
                    cast(n2, Q + (j + 2) // 4, j2, cur if j < 2 else nxt, row, first and not (tail and j >= 2))
                    past = not (first and head and j == 0)
                    if past:
                        mish_exp(g0 + j - 1, (j - 1) % 2)
                    l1 = [] if first else l1_strips(j, kind)
                    if l1:
                        off, k = l1[0]
                        relu(4 * (Q + off) + k, 0, b if head else None)
                    if tail and j == 0:
                        stats_group("x", b + 1)
                    if tail and j == 1:
                        hidden_out(b + 1)
                    if tail and j == 2:
                        bias_out(b + 1)
                    if tail and j == 3:
                        taps_high(b + 1, 1)
                    if not first and head and j == 2:
                        stats_group("1", b - 1)
                    evacuate(n2, j2, 0, row, b + 1)
                    if tail and j == 0:
                        stats_rstd("x", b + 1)
                    if not first and head and j == 2:
                        stats_rstd("1", b - 1)
                    if past:
                        mish_rest(g0 + j - 1)
                    if tail and j == 2:
                        taps_high(b + 1, 0)
                    if tail and j == 3:
                        taps_high(b + 1, 2)
                    if not first and head and j == 2:
                        layer1_bias(b - 1)
                    evacuate(n2, j2, 1, row, b + 1)
                    if l1:
                        relu(4 * (Q + off) + k, 1, None)
                    for off, k in l1[1:]:
                        for t in range(2):
                            relu(4 * (Q + off) + k, t, None)
                    if tail and j == 0:
                        pooled_out(b + 1)
                    if tail and j == 1:
                        kernels_out(b + 1)

            def epilogue():
                n = B * STRIPS
                mish_exp(n - 1, 1)
                mish_rest(n - 1)
                stats_group("1", B - 1)
                stats_rstd("1", B - 1)
                layer1_bias(B - 1)
                for s in range(STRIPS):
                    for t in range(2):
                        relu(n - STRIPS + s, t, B if s == 0 and t == 0 else None, last_bank(s, t))

            image_loop(eng, prologue, quad, epilogue)

        @block.tensor
        def _(eng):
            mm = nc.tensor.matmul

            def group_moments(who, i):
                eng.wait_ge(hk[who + "mom"], i + 1)
                mm(psM[:, 0:2], groupm[:], st[who]["agg"][:], start=True, stop=True).then_inc(hk[who + "gps"], 1)

            def pooled_products(i):
                eng.wait_ge(hk["xr"], i + 1)
                for h in range(2):
                    last = mm(psM[:, 2 * h:2 * h + 2], wint[:, h * C:(h + 1) * C], st["x"]["mm"][:],
                              start=True, stop=True)
                last.then_inc(s_pps, 1)

            def hidden(i):
                eng.wait_ge(s_pl, i + 1)
                for h in range(2):
                    for k in range(2):
                        last = mm(psM[:, h:h + 1], w1t[:, k, h * C:(h + 1) * C], pooled[:, k:k + 1],
                                  start=(k == 0), stop=(k == 1))
                last.then_inc(s_hps, 1)

            def kernels(i):
                eng.wait_ge(s_hvl, i + 1)
                for h in range(2):
                    for tap in range(TAPS):
                        o = psM[:, 2 * (h * TAPS + tap):2 * (h * TAPS + tap) + 2]
                        for k in range(2):
                            mm(o, w2p[:, 0, k, tap, h * C:(h + 1) * C], hv[:, k, 0:2], start=(k == 0), stop=False)
                            last = mm(o, w2p[:, 1, k, tap, h * C:(h + 1) * C], hv[:, k, 1:3],
                                      start=False, stop=(k == 1))
                last.then_inc(s_kps, 1)

            def bias_rows(i):
                eng.wait_ge(s_bxr, i + 1)
                eng.wait_ge(s_ksb, i + 1)
                mm(psM[0:64, 0:C], bx[:], ident[:], start=True, stop=True).then_inc(s_tps, 1)

            def spread(i, u):
                eng.wait_ge(s_kk, i + 1)
                if u == 0:
                    eng.wait_ge(s_vst, i + 1)
                else:
                    eng.wait_ge(s_wt, 3 * i + u)
                for v in range(3):
                    tap = 3 * u + v
                    last = mm(psM[:, v * C:(v + 1) * C], kk[:, tap:tap + 1].broadcast_to([C, C]), ident[:],
                              start=True, stop=True)
                last.then_inc(s_kbc, 1)

            def conv(n, j, t, tile, taps, done=False):
                r0 = 8 * j + 4 * t
                o = psA[:, j % 2, t * TP:(t + 1) * TP]
                v0 = {"first": 0, "mid": 1, "last": 2}[tile]
                if taps[0] == 0:
                    mm(o, vb[:], valid[:, v0:v0 + 4, :], start=True, stop=False)
                for tap in taps:
                    dy, dx = tap // 3, tap % 3
                    wh = wa[:, 0, tap * C:(tap + 1) * C]
                    wl = wa[:, 1, tap * C:(tap + 1) * C]
                    xhi = hi[:, r0 + dy:r0 + dy + 4, dx:dx + W]
                    xlo = lo[:, r0 + dy:r0 + dy + 4, dx:dx + W]
                    mm(o, wh, xhi, start=False, stop=False)
                    mm(o, wh, xlo, start=False, stop=False)
                    last = mm(o, wl, xhi, start=False, stop=(tap == TAPS - 1))
                if done:
                    last.then_inc(s_cv, 1)

            def product_b(n, j, t, i):
                if t == 0:
                    eng.wait_ge(s_hi, n + 1)
                    eng.wait_ge(s_lo, n + 1)
                if i is not None:
                    eng.wait_ge(s_wbh, i + 1)
                    eng.wait_ge(s_wbl, i + 1)
                if not isinstance(n, int) or n + t >= 1:
                    eng.wait_ge(s_xe, 2 * n + t)
                r0 = 8 * j + 4 * t + 1
                xhi = hi[:, r0:r0 + 4, 1:1 + W]
                xlo = lo[:, r0:r0 + 4, 1:1 + W]
                mm(psB[:], wb[:, 0, :], xhi, start=True, stop=False)
                mm(psB[:], wb[:, 0, :], xlo, start=False, stop=False)
                mm(psB[:], wb[:, 1, :], xhi, start=False, stop=True).then_inc(s_xm, 1)

            def product_out(n, t):
                if t == 0:
                    eng.wait_ge(s_w, n + 1)
                if not isinstance(n, int) or n + t >= 1:
                    eng.wait_ge(s_x1, 2 * n + t)
                for h in range(2):
                    last = mm(psO[:], woutt[:, h, :], wm[:, h * SP + t * TP:h * SP + (t + 1) * TP],
                              start=(h == 0), stop=(h == 1))
                last.then_inc(s_om, 1)

            def layer1(n, k, base, t, i, ps=None, banks=1):
                if i is not None:
                    eng.wait_ge(s_lpt, i)
                eng.wait_ge(s_re, 2 * n + t + 1 - banks + FREE)
                mm(psL[:] if ps is None else ps, lpt[:], X[:, bass.ds(base + k * SP + t * TP, TP)],
                   start=True, stop=True).then_inc(s_lm, 1)

            def layer1_mean(i):
                eng.wait_ge(hk["1r"], i + 1)
                mm(psM[:, 0:1], lt[:], st["1"]["mm"][:, 1:2], start=True, stop=True).then_inc(s_lps, 1)

            def prologue():
                eng.wait_ge(s_const, 16 * len(consts))
                mm(psM[:, 0:C], ampw, cosm, start=True, stop=True)
                mm(psM[:, C:2 * C], phw, sinm, start=True, stop=True).then_inc(s_i, 1)
                eng.wait_ge(s_j, 1)
                mm(psM[:, 0:C], cosm, m1[:, 0:C], start=True, stop=False)
                mm(psM[:, 0:C], sinm, m1[:, C:2 * C], start=False, stop=True)
                mm(psM[:, C:C + 1], cosm, ampb, start=True, stop=False)
                mm(psM[:, C:C + 1], sinm, nphb, start=False, stop=True).then_inc(s_i, 1)
                eng.wait_ge(s_j, 2)
                group_moments("x", 0)
                pooled_products(0)
                hidden(0)
                eng.wait_ge(s_w2, 2)
                kernels(0)
                bias_rows(0)
                for u in range(3):
                    spread(0, u)
                for n in range(2):
                    for t in range(2):
                        product_b(n, n, t, 0 if n + t == 0 else None)

            def quad(b, q, Q, first, kind):
                g0 = snap(eng, Q * 4)
                if not first:
                    near = snap(eng, slot(Q, -4))
                    far = snap(eng, slot(Q, -5))
                head, tail = kind == "head", kind == "tail"
                for j in range(4):
                    out_n = g0 + j - 2
                    past = not (first and head and j < 2)
                    l1 = [] if first else l1_strips(j, kind)
                    if past:
                        product_out(out_n, 0)
                    if l1:
                        off, k = l1[0]
                        layer1(4 * (Q + off) + k, k, far if off == -5 else near, 0, b if head else None)
                    if tail and j == 0:
                        group_moments("x", b + 1)
                    if tail and j == 1:
                        hidden(b + 1)
                    if tail and j == 2:
                        bias_rows(b + 1)
                    if tail and j == 3:
                        spread(b + 1, 2)
                    if not first and head and j == 2:
                        group_moments("1", b - 1)
                    if head and j == 0:
                        eng.wait_ge(s_wa, 2 * (b + 1))
                        eng.wait_ge(s_vb, b + 1)
                    if past:
                        eng.wait_ge(s_w, g0 + j - 1)
                    eng.wait_ge(s_hi, g0 + j + 2)
                    eng.wait_ge(s_lo, g0 + j + 2)
                    tile = "first" if head and j == 0 else "mid"
                    conv(g0 + j, j, 0, tile, range(3))
                    product_b(g0 + j + 2, (j + 2) % 4, 0, b + 1 if tail and j == 2 else None)
                    conv(g0 + j, j, 0, tile, range(3, TAPS))
                    if not first and head and j == 2:
                        layer1_mean(b - 1)
                    if tail and j == 1:
                        kernels(b + 1)
                    if tail and j == 2:
                        spread(b + 1, 0)
                    if past:
                        product_out(out_n, 1)
                    product_b(g0 + j + 2, (j + 2) % 4, 1, None)
                    if l1:
                        layer1(4 * (Q + off) + k, k, far if off == -5 else near, 1, None)
                    for off, k in l1[1:]:
                        for t in range(2):
                            layer1(4 * (Q + off) + k, k, far if off == -5 else near, t, None)
                    if tail and j == 0:
                        pooled_products(b + 1)
                    if tail and j == 2:
                        spread(b + 1, 1)
                    conv(g0 + j, j, 1, "last" if tail and j == 3 else "mid", range(TAPS), True)

            def epilogue():
                n = B * STRIPS
                for k in (n - 2, n - 1):
                    for t in range(2):
                        product_out(k, t)
                group_moments("1", B - 1)
                layer1_mean(B - 1)
                for s in range(STRIPS):
                    for t in range(2):
                        m = n - STRIPS + s
                        layer1(m, s % 4, slot(m // 4, 0), t, B if s == 0 and t == 0 else None, last_bank(s, t), 4)

            image_loop(eng, prologue, quad, epilogue)

        @block.vector
        def _(eng):
            V = nc.vector

            def stats_x(i, t, c, count):
                eng.wait_ge(s_sin[i], 16 * count)
                apart(eng)
                V.bn_stats(bnx[:, bass.ds(c, 1), :].rearrange("p a s -> p (a s)"), XS[:, i, :]).then_inc(s_bx, 1)

            def moments(who, i, stats, done):
                d = st[who]
                eng.wait_ge(s_bx if who == "x" else s_b1, done)
                if who == "1" or not isinstance(i, int):
                    eng.wait_ge(hk[who + "pool"], i + (who == "1"))
                apart(eng)
                V.bn_aggr(d["agg"][:], stats[:]).then_inc(hk[who + "agg"], 1)
                eng.wait_ge(hk[who + "agg"], i + 1)
                V.scalar_tensor_tensor(out=d["agg"][:, 1:2], in0=d["agg"][:, 0:1], scalar=d["agg"][:, 0:1],
                                       in1=d["agg"][:, 1:2], op0=ALU.mult, op1=ALU.add).then_inc(hk[who + "mom"], 1)

            def tap_matrices(i, u):
                eng.wait_ge(s_wn, i + 1)
                eng.wait_ge(s_kbc, 3 * i + u + 1)
                if not isinstance(i, int) or i > 0 or u > 0:
                    eng.wait_ge(s_wsl, 3 * i + u)
                V.tensor_tensor(wtmp[:].rearrange("p (k o) -> p k o", o=C),
                                psM[:, 0:3 * C].rearrange("p (k o) -> p k o", o=C),
                                wn[:, None, 0:C].broadcast_to([C, 3, C]), ALU.mult).then_inc(s_wt, 1)

            def switch_a(i, done):
                eng.wait_ge(s_wsh, 3 * i + 3)
                eng.wait_ge(s_wsl, 3 * i + 3)
                if done is not None:
                    eng.wait_ge(s_cv, done)
                V.tensor_copy(wa[:, 0, :], wst[:, 0, :]).then_inc(s_wa, 1)
                V.tensor_copy(wa[:, 1, :], wst[:, 1, :]).then_inc(s_wa, 1)
                if done is not None:
                    eng.wait_ge(s_tap, done * TAPS)
                V.tensor_copy(kb[:], kk[:, TAPS:2 * TAPS]).then_inc(s_kb, 1)
                eng.wait_ge(s_kb, i + 1)

            def tap(n, j, k):
                if k == 0:
                    eng.wait_ge(s_xe, 2 * n + 3)
                    if not isinstance(n, int) or n >= 2:
                        eng.wait_ge(s_w, n - 1)
                else:
                    eng.wait_ge(s_tap, n * TAPS + k)
                dy, dx = k // 3, k % 3
                src = xh[:, 8 * j + dy:8 * j + dy + 8, dx:dx + W]
                dst = acc[:, j % 2, :].rearrange("p (r c) -> p r c", c=W)
                if k == 0:
                    V.tensor_scalar(dst, src, kb[:, 0:1], None, ALU.mult).then_inc(s_tap, 1)
                else:
                    V.scalar_tensor_tensor(out=dst, in0=src, scalar=kb[:, k:k + 1], in1=dst,
                                           op0=ALU.mult, op1=ALU.add).then_inc(s_tap, 1)

            def bound(n):
                eng.wait_ge(s_exp, n + 1)
                V.tensor_scalar(em[:], em[:], EMAX, None, ALU.min).then_inc(s_cl, 1)

            def weigh(n, par, h):
                if h == 0:
                    eng.wait_ge(s_act, 3 * n + 3)
                    if not isinstance(n, int) or n >= 1:
                        eng.wait_ge(s_om, 2 * n)
                y = psA[:, par, :] if h == 0 else acc[:, par, :]
                last = V.scalar_tensor_tensor(out=wm[:, h * SP:(h + 1) * SP], in0=em[:, h * SP:(h + 1) * SP],
                                              scalar=0.5, in1=y, op0=ALU.subtract, op1=ALU.mult)
                if h == 1:
                    last.then_inc(s_w, 1)

            def residual(n, k, base, t):
                eng.wait_ge(s_om, 2 * n + t + 1)
                xs = X[:, bass.ds(base + k * SP + t * TP, TP)]
                V.scalar_tensor_tensor(out=xs, in0=psO[:], scalar=boutp[:, 0:1], in1=xs,
                                       op0=ALU.add, op1=ALU.add).then_inc(s_x1, 1)

            def stats_1(n, k, base, t, c):
                eng.wait_ge(s_x1, 2 * n + t + 1)
                apart(eng)
                V.bn_stats(bn1[:, bass.ds(c, 1), :].rearrange("p a s -> p (a s)"),
                           X[:, bass.ds(base + k * SP + t * TP, TP)]).then_inc(s_b1, 1)

            def prologue():
                V.memset(hi[:], 0.0).then_inc(s_zero, 1)
                V.memset(lo[:], 0.0).then_inc(s_zero, 1)
                V.memset(xh[:], 0.0).then_inc(s_zero, 1)
                V.memset(zrow[:], 0.0).then_inc(s_zero, 1)
                V.memset(bx[:], 0.0).then_inc(s_zero, 1)
                V.memset(hv[:], 0.0).then_inc(s_zero, 1)
                for c in range(2 * STRIPS):
                    if c % 2 == 0:
                        eng.wait_ge(s_first[c // 2], 16)
                    V.bn_stats(bnx[:, c, :], X[:, c * TP:(c + 1) * TP]).then_inc(s_bx, 1)
                moments("x", 0, bnx, 2 * STRIPS)
                for c in range(2 * STRIPS, 2 * STAT):
                    stats_x(c % 4, 0, c % (2 * STRIPS), c // 4 + 1 - STRIPS // 2)
                eng.wait_ge(s_const, 16 * len(consts))
                eng.wait_ge(s_w2, 1)
                V.tensor_tensor(w2p[:, 1], w2t, w2p[:, 0], ALU.subtract).then_inc(s_w2, 1)
                for u in range(3):
                    tap_matrices(0, u)

            def quad(b, q, Q, first, kind):
                g0 = snap(eng, Q * 4)
                cur = snap(eng, slot(Q, 0))
                prev = snap(eng, slot(Q, -1))
                head, tail = kind == "head", kind == "tail"
                qs = 0 if tail else q + 1
                if head:
                    switch_a(b, None if first else g0)
                if tail:
                    moments("x", b + 1, bnx, 2 * (g0 + 4))
                for j in range(4):
                    n = g0 + j
                    s1 = (j - 2) if j >= 2 else (14 + j if head else j - 2)
                    c1 = ((q * 4 + s1) * 2) if not (head and j < 2) else s1 * 2
                    base1 = cur if j >= 2 else prev
                    k1 = (j - 2) % 4
                    out_on = not (first and head and j < 2)
                    mish_on = not (first and head and j == 0)

                    def late(t):
                        if out_on:
                            residual(n - 2, k1, base1, t)

                    def ahead(t):
                        i = (2 * j + t) % 4
                        stats_x(i, t, (qs * 4 + j) * 2 + t, 2 * (Q + (STAT - STRIPS) // 4) + j // 2 + 1)

                    tap(n, j, 0)
                    ahead(0)
                    tap(n, j, 1)
                    late(0)
                    if mish_on:
                        bound(n - 1)
                    tap(n, j, 2)
                    ahead(1)
                    tap(n, j, 3)
                    if out_on:
                        stats_1(n - 2, k1, base1, 0, c1)
                    tap(n, j, 4)
                    tap(n, j, 5)
                    if tail and j == 2:
                        tap_matrices(b + 1, 0)
                    if tail and j == 3:
                        tap_matrices(b + 1, 2)
                    tap(n, j, 6)
                    if mish_on:
                        weigh(n - 1, (j - 1) % 2, 0)
                    tap(n, j, 7)
                    if mish_on:
                        weigh(n - 1, (j - 1) % 2, 1)
                    late(1)
                    tap(n, j, 8)
                    if out_on:
                        stats_1(n - 2, k1, base1, 1, c1 + 1)
                    if tail and j == 2:
                        tap_matrices(b + 1, 1)
                    if head and j == 1 and not first:
                        moments("1", b - 1, bn1, 2 * g0)

            def epilogue():
                n = B * STRIPS
                bound(n - 1)
                for t in range(2):
                    residual(n - 2, 2, slot((n - 2) // 4, 0), t)
                    stats_1(n - 2, 2, slot((n - 2) // 4, 0), t, 2 * (STRIPS - 2) + t)
                weigh(n - 1, 1, 0)
                weigh(n - 1, 1, 1)
                for t in range(2):
                    residual(n - 1, 3, slot((n - 1) // 4, 0), t)
                    stats_1(n - 1, 3, slot((n - 1) // 4, 0), t, 2 * (STRIPS - 1) + t)
                moments("1", B - 1, bn1, 2 * n)
                for s in range(STRIPS):
                    m = n - STRIPS + s
                    for t in range(2):
                        eng.wait_ge(s_re, 2 * m + t + 1 + FREE)
                        at = slot(m // 4, 0) + (s % 4) * SP + t * TP
                        V.tensor_tensor(X[:, at:at + TP], X[:, at:at + TP], zt[:, t, :], ALU.add).then_inc(s_add, 1)

            image_loop(eng, prologue, quad, epilogue)

        @block.gpsimd
        def _(eng):
            P = nc.gpsimd
            def variance(who, i, s):
                d = st[who]
                eng.wait_ge(hk[who + "gsb"], i + 1)
                P.tensor_tensor(d["t"][:], d["gm"][:, 0:1], d["gm"][:, 0:1], ALU.mult).then_inc(s, 1)
                eng.wait_ge(s, 7 * i + 1)
                P.tensor_tensor(d["t"][:], d["gm"][:, 1:2], d["t"][:], ALU.subtract).then_inc(s, 1)
                eng.wait_ge(s, 7 * i + 2)
                apart(eng)
                P.tensor_scalar(d["v"][:], d["t"][:], EPS, None, ALU.add).then_inc(hk[who + "var"], 1)

            def rstd(who, i, s):
                d = st[who]
                eng.wait_ge(hk[who + "r0"], i + 1)
                P.tensor_tensor(d["t"][:], d["r0"][:], d["r0"][:], ALU.mult).then_inc(s, 1)
                eng.wait_ge(s, 7 * i + 3)
                P.tensor_tensor(d["t"][:], d["t"][:], d["v"][:], ALU.mult).then_inc(s, 1)
                eng.wait_ge(s, 7 * i + 4)
                apart(eng)
                P.tensor_scalar(d["t"][:], d["t"][:], -0.5, 1.5, ALU.mult, ALU.add).then_inc(s, 1)
                eng.wait_ge(s, 7 * i + 5)
                P.tensor_tensor(d["r"][:], d["r0"][:], d["t"][:], ALU.mult).then_inc(s, 1)
                P.tensor_tensor(d["mm"][:, 0:1], d["agg"][:, 0:1], d["gm"][:, 0:1], ALU.subtract).then_inc(hk[who + "pool"], 1)
                eng.wait_ge(s, 7 * i + 6)
                eng.wait_ge(hk[who + "pool"], i + 1 + (who == "1"))
                P.tensor_tensor(d["mm"][:, 0:1], d["mm"][:, 0:1], d["r"][:], ALU.mult).then_inc(s, 1)
                P.tensor_tensor(d["mm"][:, 1:2], d["gm"][:, 0:1], d["r"][:], ALU.mult).then_inc(hk[who + "r"], 1)
                eng.wait_ge(s, 7 * i + 7)
                eng.wait_ge(hk[who + "r"], i + 1)

            def fold(i):
                if not isinstance(i, int) or i > 0:
                    eng.wait_ge(s_wt, 3 * i)
                apart(eng)
                P.tensor_scalar(wn[:], wint[:], st["x"]["r"][:, 0:1], None, ALU.mult).then_inc(s_wn, 1)

            def pool_bias(i):
                pv = pm[:].rearrange("p (h a) -> p a h", a=2)
                eng.wait_ge(s_psb, i + 1)
                P.tensor_tensor(pooled[:], pv[:, 0, :], binp[:], ALU.add)
                P.tensor_tensor(bp[:], binp[:], pv[:, 1, :], ALU.subtract).then_inc(s_pl, 1)

            def hidden_low(i):
                eng.wait_ge(s_hvh, i + 1)
                P.tensor_tensor(hv[:, :, 0], hcx[:], hv[:, :, 1], ALU.subtract).then_inc(s_hvl, 1)

            def kernel_bias(i):
                eng.wait_ge(s_ksb, i + 1)
                kv = kraw[:].rearrange("p (k a) -> p a k", a=2)
                P.tensor_tensor(kk[:], kv[:, 0, :], kv[:, 1, :], ALU.add).then_inc(s_ks, 1)
                eng.wait_ge(s_ks, i + 1)
                P.tensor_tensor(kk[:], kk[:], b2p[:], ALU.add).then_inc(s_kk, 1)
                eng.wait_ge(s_kk, i + 1)
                eng.wait_ge(s_pl, i + 1)
                apart(eng)
                P.tensor_scalar(bk[:], kk[:, 0:TAPS], bp[:, 0:1], None, ALU.mult).then_inc(s_bst, 1)
                eng.wait_ge(s_bst, 2 * i + 1)
                apart(eng)
                P.tensor_copy(bh[:], bk[:]).then_inc(s_bst, 1)
                eng.wait_ge(s_bst, 2 * i + 2)
                apart(eng)
                P.tensor_copy(bx[:, 0:TAPS], bh[:])
                P.tensor_tensor(bx[:, 32:32 + TAPS], bk[:], bh[:], ALU.subtract).then_inc(s_bxr, 1)

            def taps_low(i, u):
                eng.wait_ge(s_wsh, 3 * i + u + 1)
                part = slice(3 * u * C, 3 * (u + 1) * C)
                P.tensor_tensor(wst[:, 1, part], wtmp[:], wst[:, 0, part], ALU.subtract).then_inc(s_wsl, 1)

            def switch_b(i):
                eng.wait_ge(s_wbh, i + 1)
                eng.wait_ge(s_wn, i + 1)
                P.tensor_tensor(wb[:, 1, :], wn[:, C:HID], wb[:, 0, :], ALU.subtract).then_inc(s_wbl, 1)

            def fold_1(i, done):
                eng.wait_ge(s_re, done)
                apart(eng)
                P.tensor_scalar(lpt[:], lt[:], st["1"]["r"][:, 0:1], None, ALU.mult).then_inc(s_lpt, 1)

            def cast(n, j, base, row):
                eng.wait_ge(s_hi, n + 1)
                xs = X[:, bass.ds(base + j * SP, SP)].rearrange("p (r c) -> p r c", c=W)
                apart(eng)
                if row == "top":
                    P.memset(lo[:, 0, :], 0.0)
                elif row == "bottom":
                    P.memset(lo[:, RING + 1, :], 0.0)
                elif j in (0, 3):
                    p, r = (RING + 1, 0) if j == 0 else (0, ROWS - 1)
                    P.tensor_tensor(lo[:, p, 1:1 + W], xs[:, r, :], hi[:, p, 1:1 + W], ALU.subtract)
                P.tensor_tensor(lo[:, 8 * j + 1:8 * j + 9, 1:1 + W], xs,
                                hi[:, 8 * j + 1:8 * j + 9, 1:1 + W], ALU.subtract).then_inc(s_lo, 1)

            def add(n, k, base, t):
                eng.wait_ge(s_re, 2 * n + t + 1 + FREE)
                xs = X[:, bass.ds(base + k * SP + t * TP, TP)]
                P.tensor_tensor(xs, xs, zt[:, t, :], ALU.add).then_inc(s_add, 1)

            s_px, s_p1 = s_chain["x"], s_chain["1"]

            def prologue():
                eng.wait_ge(s_const, 16 * len(consts))
                eng.wait_ge(s_zero, 6)
                for t in range(FREE):
                    P.memset(bk[:], 0.0).then_inc(s_add, 1)
                    eng.wait_ge(s_add, t + 1)
                P.memset(bk[:], 0.0).then_inc(hk["1pool"], 1)
                eng.wait_ge(hk["1pool"], 1)
                variance("x", 0, s_px)
                rstd("x", 0, s_px)
                fold(0)
                pool_bias(0)
                switch_b(0)
                hidden_low(0)
                kernel_bias(0)
                for u in range(3):
                    taps_low(0, u)
                for n in range(2):
                    cast(n, n, 0, "top" if n == 0 else None)

            def quad(b, q, Q, first, kind):
                g0 = snap(eng, Q * 4)
                cur = snap(eng, slot(Q, 0))
                nxt = snap(eng, slot(Q, 1))
                near = snap(eng, slot(Q, -4))
                head, tail = kind == "head", kind == "tail"
                for j in range(4):
                    row = "bottom" if tail and j == 1 else "top" if tail and j == 2 else None
                    cast(g0 + j + 2, (j + 2) % 4, cur if j < 2 else nxt, row)
                    if tail and j == 1:
                        hidden_low(b + 1)
                    if tail and j == 2:
                        switch_b(b + 1)
                    if tail and j == 0:
                        variance("x", b + 1, s_px)
                        rstd("x", b + 1, s_px)
                        fold(b + 1)
                    if not first and head and j == 2:
                        variance("1", b - 1, s_p1)
                        rstd("1", b - 1, s_p1)
                        fold_1(b - 1, 2 * (g0 - STRIPS) + FREE)
                    if tail and j == 3:
                        taps_low(b + 1, 1)
                    l1 = [] if first else l1_strips(j, kind)
                    adds = [(off, k, t) for off, k in l1 for t in range(2)]
                    for off, k, t in adds[:1]:
                        add(4 * (Q + off) + k, k, nxt if off == -5 else near, t)
                    if tail and j == 2:
                        taps_low(b + 1, 0)
                    if tail and j == 3:
                        taps_low(b + 1, 2)
                    for off, k, t in adds[1:]:
                        add(4 * (Q + off) + k, k, nxt if off == -5 else near, t)
                    if tail and j == 0:
                        pool_bias(b + 1)
                    if tail and j == 1:
                        kernel_bias(b + 1)

            def epilogue():
                n = B * STRIPS
                variance("1", B - 1, s_p1)
                rstd("1", B - 1, s_p1)
                fold_1(B - 1, 2 * (n - STRIPS) + FREE)

            image_loop(eng, prologue, quad, epilogue)


def _layout(inputs):
    import numpy as np
    n = lambda k: np.asarray(inputs[k])
    halves = lambda v: np.ascontiguousarray(v.reshape(2, C).T)
    k_in = lambda m: np.ascontiguousarray(m.reshape(2, C, -1).transpose(1, 0, 2))
    a = {}
    a["x"] = n("x").reshape(B, C, H * W)
    a["w_in_t"] = np.ascontiguousarray(n("L0_conv_w_in").T)
    a["b_in"] = halves(n("L0_conv_b_in"))
    a["w1_t"] = k_in(n("L0_conv_kg_w1").T)
    a["b1"] = halves(n("L0_conv_kg_b1"))
    w2 = n("L0_conv_kg_w2").reshape(HID, TAPS, HID).transpose(2, 1, 0)
    a["w2_t"] = np.ascontiguousarray(w2.reshape(2, C, TAPS, HID).transpose(1, 0, 2, 3))
    a["b2"] = np.ascontiguousarray(n("L0_conv_kg_b2").reshape(2, C, TAPS).transpose(1, 0, 2).reshape(C, 2 * TAPS))
    a["w_out_t"] = k_in(n("L0_conv_w_out").T)
    a["b_out"] = n("L0_conv_b_out").reshape(C, 1)
    a["mask"] = n("L1_conv_freq_mask").reshape(C, 1)
    a["amp_w"] = n("L1_conv_amp_w")
    a["amp_b"] = n("L1_conv_amp_b").reshape(C, 1)
    a["ph_w"] = n("L1_conv_phase_w")
    a["ph_b"] = n("L1_conv_phase_b").reshape(C, 1)
    f = (np.arange(C) + C // 2) % C
    angle = 2 * np.pi * (f[:, None] * np.arange(C)[None, :] % C) / C
    a["cos_m"] = np.cos(angle).astype(np.float32)
    a["sin_m"] = np.sin(angle).astype(np.float32)
    g = np.arange(C) // GROUP
    a["group_m"] = ((g[:, None] == g[None, :]) / GROUP).astype(np.float32)
    a["ident_m"] = np.eye(C, dtype=np.float32)
    v = np.zeros((64, 6, W), np.float16)
    for tap in range(TAPS):
        dy, dx = tap // 3, tap % 3
        m = np.ones((6, W))
        if dy == 0:
            m[0] = 0
        if dy == 2:
            m[5] = 0
        if dx == 0:
            m[:, 0] = 0
        if dx == 2:
            m[:, W - 1] = 0
        v[tap] = v[32 + tap] = m
    a["valid_m"] = v
    return a


def kernel(**inputs):
    import numpy as _np
    import concourse.bacc as _bacc
    from concourse.bass_utils import run_bass_kernel_spmd as _run

    nc = _bacc.Bacc("TRN2", target_bir_lowering=False, num_devices=1)
    arrays, args = {}, {}
    for name, a in _layout(inputs).items():
        arrays[f"in_{name}_dram"] = a
        args[name] = nc.dram_tensor(f"in_{name}_dram", a.shape, mybir.dt.from_np(a.dtype), kind="ExternalInput").ap()
    out = nc.dram_tensor("out_0_dram", (B, C, H * W), F32, kind="ExternalOutput").ap()
    conv_preact_kernel(nc, out=out, **args)
    r = _run(nc, [arrays], core_ids=[0])
    return r.results[0]["out_0_dram"].reshape(B, C, H, W)
```

```python
import concourse.bass as bass
from concourse import mybir
from contextlib import ExitStack

F32 = mybir.dt.float32
F16 = mybir.dt.float16
ALU = mybir.AluOpType
ACT = mybir.ActivationFunctionType

B, C, H, W = 16, 128, 128, 128
HID = 2 * C
TAPS = 9
ROWS = 8
SP = ROWS * W
TP = SP // 2
STRIPS = H // ROWS
QUADS = STRIPS // 4
PW = W + 2
RING = 32
XG = 6
AHEAD = 4
SIDE = 14
STAT = 20
LOADED = STAT + 1
GROUP = 4
EPS = 1e-5
EMAX = float(2 ** 30)


def conv_preact_kernel(nc, x, w_in_t, b_in, w1_t, b1, w2_t, b2, w_out_t, b_out, mask, amp_w, amp_b,
                       ph_w, ph_b, cos_m, sin_m, group_m, ident_m, valid_m, out):
    ctx = ExitStack()
    with ctx:
        def sb(name, shape, dt=F32):
            return ctx.enter_context(nc.sbuf_tensor(name, shape, dt))

        def pb(name, shape):
            return ctx.enter_context(nc.psum_tensor(name, shape, F32))

        def sem(name):
            return ctx.enter_context(nc.semaphore(name))

        vectors = sb("vectors", [C, 332])
        taken = [0]

        def few(n):
            taken[0] += n
            return vectors[:, taken[0] - n:taken[0]]

        X = sb("X", [C, XG * 4 * SP])
        XS = sb("XS", [C, SP])
        hi = sb("hi", [C, RING + 2, PW], F16)
        lo = sb("lo", [C, RING + 2, PW], F16)
        xh = sb("xh", [C, RING + 2, PW])
        acc = sb("acc", [C, 2, SP])
        side = sb("side", [C, RING + 2, SIDE + 2])
        sacc = sb("sacc", [C, ROWS, SIDE])
        junk = sb("junk", [C, SP], F16)
        em = sb("em", [C, 2 * SP])
        wm = sb("wm", [C, 2 * SP])
        zt = sb("zt", [C, 2, TP])
        w2p = sb("w2p", [C, 2, 2, TAPS, HID], F16)
        w1t = sb("w1t", [C, 2, HID])
        wint = sb("wint", [C, HID])
        wn = sb("wn", [C, HID])
        woutt = sb("woutt", [C, 2, C])
        ident = sb("ident", [C, C])
        groupm = sb("groupm", [C, C])
        lt = sb("lt", [C, C])
        lpt = sb("lpt", [C, C])
        valid = sb("valid", [64, 6, W], F16)
        wst = sb("wst", [C, 2, TAPS * C], F16)
        wa = sb("wa", [C, 2, TAPS * C], F16)
        wtmp = sb("wtmp", [C, 3 * C])
        wb = sb("wb", [C, 2, HID], F16)
        vbst = sb("vbst", [64, C], F16)
        vb = sb("vb", [64, C], F16)
        bx = sb("bx", [C, 64])
        bh = sb("bh", [C, TAPS], F16)
        hv = sb("hv", [C, 2, 4], F16)
        bk = few(TAPS)
        zrow = sb("zrow", [C, PW], F16)
        binp = few(2)
        b1p = few(2)
        b2p = few(2 * TAPS)
        boutp = few(1)
        spare = few(4)
        cl = few(1)
        lb = few(1)
        bpl = few(2)
        sumx, sqx = few(STRIPS), few(STRIPS)
        sum1, sq1 = few(2 * STRIPS), few(STRIPS)
        kk = few(2 * TAPS)
        kb = few(2 * TAPS)
        pooled = few(2)
        bp = few(2)
        pm = few(4)
        hcx = few(2)
        kraw = few(4 * TAPS)
        st = {}
        for who in ("x", "1"):
            st[who] = {k: few(n) for k, n in
                       (("agg", 2), ("gm", 2), ("t", 1), ("v", 1), ("ln", 1), ("r0", 1), ("r", 1), ("mm", 2),
                        ("junk", 3 * STRIPS))}

        bnx = wm[:, 0:12 * STRIPS].rearrange("p (t s) -> p t s", s=6)
        w2t = X[:, STRIPS * SP:STRIPS * SP + 2 * TAPS * HID].rearrange("p (k t o) -> p k t o", k=2, t=TAPS)
        cosm, sinm, ampw, phw = (em[:, i * C:(i + 1) * C] for i in range(4))
        m1 = em[:, 4 * C:6 * C]
        small = em[:, 6 * C:6 * C + 4]
        maskp, ampb, phb, nphb = (small[:, i:i + 1] for i in range(4))

        psA = pb("psA", [C, 2, SP])
        psB = pb("psB", [C, TP])
        psO = pb("psO", [C, TP])
        psL = pb("psL", [C, TP])
        psM = pb("psM", [C, TP])

        s_const = sem("s_const")
        s_xin = [sem(f"s_xin{j}") for j in range(4)]
        s_first = [sem(f"s_first{n}") for n in range(STRIPS)]
        s_sin = sem("s_sin")
        s_out = [sem(f"s_out{j}") for j in range(4)]
        s_zero = sem("s_zero")
        s_hi = sem("s_hi")
        s_lo = sem("s_lo")
        s_xm = sem("s_xm")
        s_xe = sem("s_xe")
        s_cv = sem("s_cv")
        s_tap = sem("s_tap")
        s_st = sem("s_st")
        s_exp = sem("s_exp")
        s_cl = sem("s_cl")
        s_act = sem("s_act")
        s_w = sem("s_w")
        s_om = sem("s_om")
        s_x1 = sem("s_x1")
        s_lm = sem("s_lm")
        s_re = sem("s_re")
        s_add = sem("s_add")
        s_b0 = sem("s_b0")
        s_sx = sem("s_sx")
        s_bx = sem("s_bx")
        s_b1 = sem("s_b1")
        hk = {}
        for who in ("x", "1"):
            for k in ("agg", "mom", "gps", "gsb", "var", "ln", "r0", "r", "pool"):
                hk[who + k] = sem(f"s_{who}_{k}")
        s_wn = sem("s_wn")
        s_pps = sem("s_pps")
        s_psb = sem("s_psb")
        s_pl = sem("s_pl")
        s_hps = sem("s_hps")
        s_hcx = sem("s_hcx")
        s_hvh = sem("s_hvh")
        s_hvl = sem("s_hvl")
        s_ks = sem("s_ks")
        s_w2 = sem("s_w2")
        s_kps = sem("s_kps")
        s_ksb = sem("s_ksb")
        s_kk = sem("s_kk")
        s_bxr = sem("s_bxr")
        s_bst = sem("s_bst")
        s_tps = sem("s_tps")
        s_vst = sem("s_vst")
        s_kbc = sem("s_kbc")
        s_wt = sem("s_wt")
        s_wsh = sem("s_wsh")
        s_wsl = sem("s_wsl")
        s_wa = sem("s_wa")
        s_vb = sem("s_vb")
        s_kb = sem("s_kb")
        s_wbh = sem("s_wbh")
        s_wbl = sem("s_wbl")
        s_bpl = sem("s_bpl")
        s_lps = sem("s_lps")
        s_lpt = sem("s_lpt")
        s_lb = sem("s_lb")
        s_i = sem("s_i")
        s_j = sem("s_j")
        s_chain = {who: sem(f"s_chain_{who}") for who in ("x", "1")}

        s_apart = sem("s_apart")

        consts = [
            (cosm, cos_m), (sinm, sin_m), (ampw, amp_w), (phw, ph_w), (maskp, mask), (ampb, amp_b),
            (phb, ph_b), (groupm[:], group_m), (ident[:], ident_m), (valid[:], valid_m), (wint[:], w_in_t),
            (binp[:], b_in), (b1p[:], b1), (b2p[:], b2), (boutp[:], b_out), (w1t[:], w1_t),
            (woutt[:], w_out_t), (w2t, w2_t),
        ]

        block = ctx.enter_context(nc.Block())

        FREE = 2

        def snap(eng, v):
            return v if isinstance(v, int) else eng.snap(v)

        def apart(eng):
            eng.sem_inc(s_apart, 1)

        def last_bank(s, t):
            return psA[:, s % 2, t * TP:(t + 1) * TP]

        def slot(Q, k):
            return ((Q + (k % XG)) % XG) * (4 * SP)

        def image_loop(eng, prologue, quad, epilogue):
            prologue()
            for era in range(3):
                def image(b):
                    quad(b, 0, b * QUADS, era, "head")
                    with eng.Fori(1, QUADS - 1) as q:
                        quad(b, q, b * QUADS + q, era, "mid")
                    quad(b, QUADS - 1, b * QUADS + QUADS - 1, era, "tail")
                if era < 2:
                    image(era)
                else:
                    with eng.Fori(2, B) as b:
                        image(b)
            epilogue()

        def l1_strip(j, kind, era):
            if era == 0 or (era == 1 and kind == "head" and j < 3):
                return None
            return (-5, j + 1) if j < 3 else (-4, 0)

        @block.sync
        def _(eng):
            xr = x.rearrange("b c n -> c b n")
            outr = out.rearrange("b c n -> c b n")

            def load_x(n4, j, b, px, base, free, used):
                if free is not None:
                    eng.wait_ge(s_out[j], free)
                    apart(eng)
                if used is not None:
                    eng.wait_ge(s_hi, used)
                apart(eng)
                eng.dma_start(X[:, bass.ds(base + j * SP, SP)], xr[:, bass.ds(b, 1), bass.ds(px, SP)]
                              .rearrange("c b n -> c (b n)")).then_inc(s_xin[j], 16)

            def load_stat(b, px, used):
                if used is not None:
                    eng.wait_ge(s_bx, used)
                apart(eng)
                eng.dma_start(XS[:], xr[:, bass.ds(b, 1), bass.ds(px, SP)]
                              .rearrange("c b n -> c (b n)")).then_inc(s_sin, 16)

            def store(k, j, b, px, base, n):
                eng.wait_ge(s_add, 2 * n + 2 + FREE)
                apart(eng)
                eng.wait_ge(s_out[j], 16 * (k + 1))
                apart(eng)
                eng.dma_start(outr[:, bass.ds(b, 1), bass.ds(px, SP)].rearrange("c b n -> c (b n)"),
                              X[:, bass.ds(base + j * SP, SP)]).then_inc(s_out[j], 16)

            def constants():
                for j in range(4):
                    eng.dma_start(spare[:, j:j + 1], b_out).then_inc(s_out[j], 16)
                for dst, src in consts:
                    eng.dma_start(dst, src).then_inc(s_const, 16)

            def prologue():
                for n in range(STRIPS):
                    eng.dma_start(X[:, n * SP:(n + 1) * SP], xr[:, 0, n * SP:(n + 1) * SP]).then_inc(s_first[n], 16)
                    if n == 1:
                        constants()
                for n in range(STRIPS, LOADED):
                    load_stat(1, (n - STRIPS) * SP, n - STRIPS if n > STRIPS else None)

            def quad(b, q, Q, era, kind):
                first = era == 0
                g0 = snap(eng, Q * 4)
                nxt = snap(eng, slot(Q, 1))
                old = snap(eng, slot(Q, -4))
                bl = snap(eng, (b + (1 if kind == "tail" else 0)) % B)
                ql = 0 if kind == "tail" else q + 1
                for j in range(4):
                    l1 = l1_strip(j, kind, era)
                    if l1:
                        off, k = l1
                        before = kind == "head" and off == -5
                        qq = q + off + QUADS * (2 if before else 1)
                        store(Q + off, k, b - (2 if before else 1), (qq * 4 + k) * SP,
                              nxt if off == -5 else old, (Q + off) * 4 + k)
                    if not (first and kind != "tail"):
                        load_x(Q + 1, j, bl, (ql * 4 + j) * SP, nxt, None if first else 16 * (Q - 3), g0 + j + 1)
                    ns = snap(eng, g0 + j + LOADED)
                    load_stat((ns // STRIPS) % B, (ns % STRIPS) * SP, ns - STRIPS)

            def epilogue():
                for n in range(B * STRIPS - STRIPS - 3, B * STRIPS):
                    store(n // 4, n % 4, n // STRIPS, n % STRIPS * SP, slot(n // 4, 0), n)
                for j in range(4):
                    eng.wait_ge(s_out[j], 16 * (B * QUADS + 1))

            image_loop(eng, prologue, quad, epilogue)
            for j in range(4):
                eng.wait_ge(s_xin[j], 16 * (B * QUADS + 1 - QUADS))
            eng.wait_ge(s_sin, 16 * (B * STRIPS + LOADED - STRIPS))

        @block.scalar
        def _(eng):
            act = nc.scalar.activation

            def stats_group(who, i):
                eng.wait_ge(hk[who + "gps"], i + 1)
                act(st[who]["gm"][:], psM[:, 0:2], ACT.Copy).then_inc(hk[who + "gsb"], 1)

            def stats_rstd(who, i):
                d = st[who]
                eng.wait_ge(hk[who + "var"], i + 1)
                act(d["ln"][:], d["v"][:], ACT.Ln).then_inc(hk[who + "ln"], 1)
                eng.wait_ge(hk[who + "ln"], i + 1)
                act(d["r0"][:], d["ln"][:], ACT.Exp, scale=-0.5).then_inc(hk[who + "r0"], 1)

            def pooled_out(i):
                eng.wait_ge(s_pps, i + 1)
                act(pm[:], psM[:, 0:4], ACT.Copy).then_inc(s_psb, 1)

            def hidden_out(i):
                eng.wait_ge(s_hps, i + 1)
                for h in range(2):
                    last = act(hcx[:, h:h + 1], psM[:, h:h + 1], ACT.Relu, bias=b1p[:, h:h + 1])
                last.then_inc(s_hcx, 1)
                eng.wait_ge(s_hcx, i + 1)
                act(hv[:, :, 1], hcx[:], ACT.Copy).then_inc(s_hvh, 1)

            def kernels_out(i):
                eng.wait_ge(s_kps, i + 1)
                act(kraw[:], psM[:, 0:4 * TAPS], ACT.Copy).then_inc(s_ksb, 1)

            def bias_out(i):
                eng.wait_ge(s_tps, i + 1)
                act(vbst[:], psM[0:64, 0:C], ACT.Copy).then_inc(s_vst, 1)

            def taps_high(i, u):
                eng.wait_ge(s_wt, 3 * i + u + 1)
                act(wst[:, 0, 3 * u * C:3 * (u + 1) * C], wtmp[:], ACT.Copy).then_inc(s_wsh, 1)

            def switch_b(i, done):
                if done is not None:
                    eng.wait_ge(s_xm, done)
                eng.wait_ge(s_wn, i + 1)
                act(wb[:, 0, :], wn[:], ACT.Copy).then_inc(s_wbh, 1)
                if done is not None:
                    eng.wait_ge(s_xe, done)
                eng.wait_ge(s_pl, i + 1)
                act(bpl[:], bp[:], ACT.Copy).then_inc(s_bpl, 1)

            def switch_a(i, done):
                if done is not None:
                    eng.wait_ge(s_cv, done)
                eng.wait_ge(s_vst, i + 1)
                act(vb[:], vbst[:], ACT.Copy).then_inc(s_vb, 1)

            def cast(n, n4, j, base, row, there):
                if not there:
                    eng.wait_ge(s_xin[j], 16 * (n4 + 1 - QUADS))
                if not isinstance(n, int) or n >= 3:
                    eng.wait_ge(s_cv, n - 2)
                xs = X[:, bass.ds(base + j * SP, SP)].rearrange("p (r c) -> p r c", c=W)
                edge_row(eng, hi, j, row, lambda r: xs[:, r * (ROWS - 1), :])
                act(hi[:, 8 * j + 1:8 * j + 9, 1:1 + W], xs, ACT.Copy).then_inc(s_hi, 1)

            def edge_row(eng, ring, j, row, src, bias=None):
                pw = ring.shape[2]
                if row == "top":
                    act(ring[:, 0, :], zrow[:, 0:pw], ACT.Copy)
                elif row == "bottom":
                    act(ring[:, RING + 1, :], zrow[:, 0:pw], ACT.Copy)
                elif j == 0 or j == 3:
                    dst = ring[:, RING + 1 if j == 0 else 0, 1:(1 + W if pw == PW else pw)]
                    r = 0 if j == 0 else 1
                    if bias is None:
                        act(dst, src(r), ACT.Copy)
                    else:
                        act(dst, src(r), ACT.Identity, bias=bias)

            def evacuate(n, j, t, row, i):
                eng.wait_ge(s_xm, 3 * n + t + 1)
                if t == 0:
                    if not isinstance(n, int) or n >= 3:
                        eng.wait_ge(s_tap, (n - 2) * TAPS)
                    if row == "top":
                        eng.wait_ge(s_bpl, i + 1)
                ps = psB[:].rearrange("p (r c) -> p r c", c=W)
                if (j == 0 and t == 0) or (j == 3 and t == 1):
                    edge_row(eng, xh, j, row, lambda r: ps[:, r * 3, :], bias=bpl[:, 1:2])
                r0 = 8 * j + 4 * t + 1
                act(xh[:, r0:r0 + 4, 1:1 + W], ps, ACT.Identity, bias=bpl[:, 1:2]).then_inc(s_xe, 1)

            def evacuate_side(n, j, row):
                eng.wait_ge(s_xm, 3 * n + 3)
                if not isinstance(n, int) or n >= 3:
                    eng.wait_ge(s_st, (n - 2) * TAPS)
                ps = psB[:, 0:ROWS * (SIDE + 1)].rearrange("p (r c) -> p r c", c=SIDE + 1)
                edge_row(eng, side, j, row, lambda r: ps[:, r * (ROWS - 1), :], bias=bpl[:, 0:1])
                act(side[:, 8 * j + 1:8 * j + 9, 1:2 + SIDE], ps, ACT.Identity, bias=bpl[:, 0:1]).then_inc(s_xe, 1)

            def sums_x(s, count, squares):
                eng.wait_ge(s_sin, 16 * count)
                if squares is not None:
                    eng.wait_ge(s_b1, squares)
                elif not isinstance(count, int) or count > 1:
                    eng.wait_ge(s_bx, count - 1)
                act(junk[:], XS[:], ACT.Copy, accum_out=sumx[:, bass.ds(s, 1)]).then_inc(s_sx, 1)
                eng.wait_ge(s_sx, count)
                act(junk[:], XS[:], ACT.Square, accum_out=sqx[:, bass.ds(s, 1)]).then_inc(s_bx, 1)

            def squares_1(n, k, base, s, sums):
                eng.wait_ge(s_x1, 2 * n + 2)
                eng.wait_ge(s_bx, sums)
                act(junk[:], X[:, bass.ds(base + k * SP, SP)], ACT.Square,
                    accum_out=sq1[:, bass.ds(s, 1)]).then_inc(s_b1, 1)

            def moments(who, i, done):
                sums, squares = (sumx, sqx) if who == "x" else (sum1, sq1)
                agg = st[who]["agg"]
                eng.wait_ge(s_bx if who == "x" else s_b1, done)
                eng.wait_ge(hk[who + "pool"], i + (who == "1"))
                few_junk = st[who]["junk"]
                act(few_junk[:, 0:sums.shape[1]], sums[:], ACT.Copy, scale=1.0 / (H * W), accum_out=agg[:, 0:1])
                act(few_junk[:, 2 * STRIPS:], squares[:], ACT.Copy, scale=1.0 / (H * W),
                    accum_out=agg[:, 1:2]).then_inc(hk[who + "mom"], 1)

            def mish_exp(n, par):
                if not isinstance(n, int) or n >= 1:
                    eng.wait_ge(s_w, n)
                eng.wait_ge(s_cv, n + 1)
                eng.wait_ge(s_st, (n + 1) * TAPS)
                act(em[:, 0:SP], psA[:, par, :], ACT.Exp)
                eng.wait_ge(s_tap, (n + 1) * TAPS)
                act(em[:, SP:2 * SP], acc[:, par, :], ACT.Exp).then_inc(s_exp, 1)

            def mish_rest(n):
                eng.wait_ge(s_cl, n + 1)
                act(em[:], em[:], ACT.Square, bias=1.0).then_inc(s_act, 1)
                eng.wait_ge(s_act, 3 * n + 1)
                act(em[:], em[:], ACT.Ln, bias=1.0).then_inc(s_act, 1)
                eng.wait_ge(s_act, 3 * n + 2)
                act(em[:], em[:], ACT.Exp, scale=-1.0).then_inc(s_act, 1)

            def relu(n, t, i, ps=None):
                if i is not None:
                    eng.wait_ge(s_lb, i)
                eng.wait_ge(s_lm, 2 * n + t + 1)
                eng.wait_ge(s_add, 2 * n + t - 1 + FREE)
                act(zt[:, t, :], psL[:] if ps is None else ps, ACT.Relu, bias=lb[:, 0:1]).then_inc(s_re, 1)

            def layer1_bias(i):
                eng.wait_ge(s_lps, i + 1)
                eng.wait_ge(s_re, 2 * STRIPS * i + FREE)
                act(lb[:], psM[:, 0:1], ACT.Identity, bias=cl[:, 0:1], scale=-1.0).then_inc(s_lb, 1)

            def prologue():
                nc.scalar.preload_act_table_set("natural_log_exp_and_others")
                eng.wait_ge(s_const, 16 * len(consts))
                eng.wait_ge(s_i, 1)
                act(m1[:, 0:C], psM[:, 0:C], ACT.Copy, scale=maskp)
                act(m1[:, C:2 * C], psM[:, C:2 * C], ACT.Copy, scale=maskp)
                act(nphb, phb, ACT.Copy, scale=-1.0).then_inc(s_j, 1)
                eng.wait_ge(s_i, 2)
                act(lt[:], psM[:, 0:C], ACT.Copy, scale=1.0 / C)
                act(cl[:], psM[:, C:C + 1], ACT.Copy, scale=1.0 / C)
                act(woutt[:], woutt[:], ACT.Copy, scale=-2.0).then_inc(s_j, 1)
                eng.wait_ge(s_j, 2)
                eng.wait_ge(s_zero, 7)
                for t in range(FREE):
                    act(zt[:, t, 0:PW], zrow[:], ACT.Copy).then_inc(s_re, 1)
                act(w2p[:, 0], w2t, ACT.Copy).then_inc(s_w2, 1)
                stats_group("x", 0)
                stats_rstd("x", 0)
                pooled_out(0)
                switch_b(0, None)
                hidden_out(0)
                kernels_out(0)
                bias_out(0)
                for u in range(3):
                    taps_high(0, u)
                for n in range(2):
                    cast(n, 0, n, 0, "top" if n == 0 else None, True)
                for n in range(2):
                    for t in range(2):
                        evacuate(n, n, t, "top" if n == 0 else None, 0)
                    evacuate_side(n, n, "top" if n == 0 else None)
                for s in range(STAT - STRIPS):
                    sums_x(s, s + 1, None)

            def quad(b, q, Q, era, kind):
                first = era == 0
                g0 = snap(eng, Q * 4)
                prev = snap(eng, slot(Q, -1))
                cur = snap(eng, slot(Q, 0))
                nxt = snap(eng, slot(Q, 1))
                for j in range(4):
                    head, tail = kind == "head", kind == "tail"
                    if tail and j == 0:
                        moments("x", b + 1, g0 + STAT - STRIPS)
                    if head and j == 0:
                        switch_a(b, None if first else g0)
                    if tail and j == 2:
                        switch_b(b + 1, 3 * (g0 + 4))
                    j2 = (j + 2) % 4
                    n2 = g0 + j + 2
                    row = "bottom" if tail and j == 1 else "top" if tail and j == 2 else None
                    cast(n2, Q + (j + 2) // 4, j2, cur if j < 2 else nxt, row, first and not (tail and j >= 2))
                    past = not (first and head and j == 0)
                    if past:
                        mish_exp(g0 + j - 1, (j - 1) % 2)
                    l1 = l1_strip(j, kind, era)
                    if l1:
                        off, k = l1
                        relu(4 * (Q + off) + k, 0, b if head and j == 3 else None)
                    if tail and j == 0:
                        stats_group("x", b + 1)
                    if tail and j == 1:
                        hidden_out(b + 1)
                    if tail and j == 2:
                        bias_out(b + 1)
                    if tail and j == 3:
                        taps_high(b + 1, 1)
                    if not first and head and j == 2:
                        stats_group("1", b - 1)
                    evacuate(n2, j2, 0, row, b + 1)
                    if tail and j == 0:
                        stats_rstd("x", b + 1)
                    if not first and head and j == 2:
                        stats_rstd("1", b - 1)
                    if past:
                        mish_rest(g0 + j - 1)
                    if tail and j == 2:
                        taps_high(b + 1, 0)
                    if tail and j == 3:
                        taps_high(b + 1, 2)
                    evacuate(n2, j2, 1, row, b + 1)
                    if l1:
                        relu(4 * (Q + off) + k, 1, None)
                    if not first and head and j == 2:
                        layer1_bias(b - 1)
                    if tail and j == 0:
                        pooled_out(b + 1)
                    if tail and j == 1:
                        kernels_out(b + 1)
                    summed = g0 + j + STAT - STRIPS
                    if j == 3:
                        squares_1(g0, 0, cur, 4 * q, summed)
                    elif not head:
                        squares_1(g0 + j - 3, j + 1, prev, 4 * q + j - 3, summed)
                    elif not first and j < 2:
                        squares_1(g0 + j - 3, j + 1, prev, STRIPS + j - 3, summed)
                    sums_x((0 if tail else 4 * q + 4) + j, summed + 1,
                           None if first and head and j < 3 else g0 + j - 2)
                    if not first and head and j == 1:
                        squares_1(g0 - 1, 3, prev, STRIPS - 1, summed + 1)
                        moments("1", b - 1, g0)
                    evacuate_side(n2, j2, row)

            def epilogue():
                n = B * STRIPS
                mish_exp(n - 1, 1)
                for m in range(n - STRIPS - 3, n - STRIPS):
                    for t in range(2):
                        relu(m, t, None)
                mish_rest(n - 1)
                for k in range(n - 3, n):
                    squares_1(k, k % 4, slot(k // 4, 0), k % STRIPS, n + STAT - STRIPS)
                    if k < n - 1:
                        eng.wait_ge(s_b1, k + 1)
                moments("1", B - 1, n)
                stats_group("1", B - 1)
                stats_rstd("1", B - 1)
                layer1_bias(B - 1)
                for s in range(STRIPS):
                    for t in range(2):
                        relu(n - STRIPS + s, t, B if s == 0 and t == 0 else None, last_bank(s, t))

            image_loop(eng, prologue, quad, epilogue)

        @block.tensor
        def _(eng):
            mm = nc.tensor.matmul

            def group_moments(who, i):
                eng.wait_ge(hk[who + "mom"], i + 1)
                mm(psM[:, 0:2], groupm[:], st[who]["agg"][:], start=True, stop=True).then_inc(hk[who + "gps"], 1)

            def pooled_products(i):
                eng.wait_ge(hk["xr"], i + 1)
                for h in range(2):
                    last = mm(psM[:, 2 * h:2 * h + 2], wint[:, h * C:(h + 1) * C], st["x"]["mm"][:],
                              start=True, stop=True)
                last.then_inc(s_pps, 1)

            def hidden(i):
                eng.wait_ge(s_pl, i + 1)
                for h in range(2):
                    for k in range(2):
                        last = mm(psM[:, h:h + 1], w1t[:, k, h * C:(h + 1) * C], pooled[:, k:k + 1],
                                  start=(k == 0), stop=(k == 1))
                last.then_inc(s_hps, 1)

            def kernels(i):
                eng.wait_ge(s_hvl, i + 1)
                for h in range(2):
                    for tap in range(TAPS):
                        o = psM[:, 2 * (h * TAPS + tap):2 * (h * TAPS + tap) + 2]
                        for k in range(2):
                            mm(o, w2p[:, 0, k, tap, h * C:(h + 1) * C], hv[:, k, 0:2], start=(k == 0), stop=False)
                            last = mm(o, w2p[:, 1, k, tap, h * C:(h + 1) * C], hv[:, k, 1:3],
                                      start=False, stop=(k == 1))
                last.then_inc(s_kps, 1)

            def bias_rows(i):
                eng.wait_ge(s_bxr, i + 1)
                eng.wait_ge(s_ksb, i + 1)
                mm(psM[0:64, 0:C], bx[:], ident[:], start=True, stop=True).then_inc(s_tps, 1)

            def spread(i, u):
                eng.wait_ge(s_kk, i + 1)
                if u == 0:
                    eng.wait_ge(s_vst, i + 1)
                else:
                    eng.wait_ge(s_wt, 3 * i + u)
                for v in range(3):
                    tap = 3 * u + v
                    last = mm(psM[:, v * C:(v + 1) * C], kk[:, tap:tap + 1].broadcast_to([C, C]), ident[:],
                              start=True, stop=True)
                last.then_inc(s_kbc, 1)

            def conv(n, j, t, tile, taps, done=False):
                r0 = 8 * j + 4 * t
                o = psA[:, j % 2, t * TP:(t + 1) * TP].rearrange("p (r c) -> p r c", c=W)[:, :, SIDE:W]
                v0 = {"first": 0, "mid": 1, "last": 2}[tile]
                if taps[0] == 0:
                    mm(o, vb[:], valid[:, v0:v0 + 4, SIDE:W], start=True, stop=False)
                for tap in taps:
                    dy, dx = tap // 3, tap % 3
                    wh = wa[:, 0, tap * C:(tap + 1) * C]
                    wl = wa[:, 1, tap * C:(tap + 1) * C]
                    xhi = hi[:, r0 + dy:r0 + dy + 4, SIDE + dx:dx + W]
                    xlo = lo[:, r0 + dy:r0 + dy + 4, SIDE + dx:dx + W]
                    mm(o, wh, xhi, start=False, stop=False)
                    mm(o, wh, xlo, start=False, stop=False)
                    last = mm(o, wl, xhi, start=False, stop=(tap == TAPS - 1))
                if done:
                    last.then_inc(s_cv, 1)

            def product_b(n, j, t, i):
                if t == 0:
                    eng.wait_ge(s_hi, n + 1)
                    eng.wait_ge(s_lo, n + 1)
                if i is not None:
                    eng.wait_ge(s_wbh, i + 1)
                    eng.wait_ge(s_wbl, i + 1)
                if not isinstance(n, int) or n + t >= 1:
                    eng.wait_ge(s_xe, 3 * n + t)
                r0 = 8 * j + 4 * t + 1
                xhi = hi[:, r0:r0 + 4, 1:1 + W]
                xlo = lo[:, r0:r0 + 4, 1:1 + W]
                mm(psB[:], wb[:, 0, C:HID], xhi, start=True, stop=False)
                mm(psB[:], wb[:, 0, C:HID], xlo, start=False, stop=False)
                mm(psB[:], wb[:, 1, C:HID], xhi, start=False, stop=True).then_inc(s_xm, 1)

            def product_side(n, j):
                eng.wait_ge(s_xe, 3 * n + 2)
                o = psB[:, 0:ROWS * (SIDE + 1)]
                xhi = hi[:, 8 * j + 1:8 * j + 9, 1:2 + SIDE]
                xlo = lo[:, 8 * j + 1:8 * j + 9, 1:2 + SIDE]
                mm(o, wb[:, 0, 0:C], xhi, start=True, stop=False)
                mm(o, wb[:, 0, 0:C], xlo, start=False, stop=False)
                mm(o, wb[:, 1, 0:C], xhi, start=False, stop=True).then_inc(s_xm, 1)

            def product_out(n, t):
                if t == 0:
                    eng.wait_ge(s_w, n + 1)
                if not isinstance(n, int) or n + t >= 1:
                    eng.wait_ge(s_x1, 2 * n + t)
                for h in range(2):
                    last = mm(psO[:], woutt[:, h, :], wm[:, h * SP + t * TP:h * SP + (t + 1) * TP],
                              start=(h == 0), stop=(h == 1))
                last.then_inc(s_om, 1)

            def layer1(n, k, base, t, i, ps=None, banks=1):
                if i is not None:
                    eng.wait_ge(s_lpt, i)
                eng.wait_ge(s_re, 2 * n + t + 1 - banks + FREE)
                mm(psL[:] if ps is None else ps, lpt[:], X[:, bass.ds(base + k * SP + t * TP, TP)],
                   start=True, stop=True).then_inc(s_lm, 1)

            def layer1_mean(i):
                eng.wait_ge(hk["1r"], i + 1)
                mm(psM[:, 0:1], lt[:], st["1"]["mm"][:, 1:2], start=True, stop=True).then_inc(s_lps, 1)

            def prologue():
                eng.wait_ge(s_const, 16 * len(consts))
                mm(psM[:, 0:C], ampw, cosm, start=True, stop=True)
                mm(psM[:, C:2 * C], phw, sinm, start=True, stop=True).then_inc(s_i, 1)
                eng.wait_ge(s_j, 1)
                mm(psM[:, 0:C], cosm, m1[:, 0:C], start=True, stop=False)
                mm(psM[:, 0:C], sinm, m1[:, C:2 * C], start=False, stop=True)
                mm(psM[:, C:C + 1], cosm, ampb, start=True, stop=False)
                mm(psM[:, C:C + 1], sinm, nphb, start=False, stop=True).then_inc(s_i, 1)
                eng.wait_ge(s_j, 2)
                group_moments("x", 0)
                pooled_products(0)
                hidden(0)
                eng.wait_ge(s_w2, 2)
                kernels(0)
                bias_rows(0)
                for u in range(3):
                    spread(0, u)
                for n in range(2):
                    for t in range(2):
                        product_b(n, n, t, 0 if n + t == 0 else None)
                    product_side(n, n)

            def quad(b, q, Q, era, kind):
                first = era == 0
                g0 = snap(eng, Q * 4)
                if not first:
                    near = snap(eng, slot(Q, -4))
                    far = snap(eng, slot(Q, -5))
                head, tail = kind == "head", kind == "tail"
                for j in range(4):
                    out_n = g0 + j - 2
                    past = not (first and head and j < 2)
                    l1 = l1_strip(j, kind, era)
                    if past:
                        product_out(out_n, 0)
                    if l1:
                        off, k = l1
                        layer1(4 * (Q + off) + k, k, far if off == -5 else near, 0,
                               b if head and j == 3 else None)
                    if tail and j == 0:
                        group_moments("x", b + 1)
                    if tail and j == 1:
                        hidden(b + 1)
                    if tail and j == 2:
                        bias_rows(b + 1)
                    if tail and j == 3:
                        spread(b + 1, 2)
                    if not first and head and j == 2:
                        group_moments("1", b - 1)
                    if head and j == 0:
                        eng.wait_ge(s_wa, 2 * (b + 1))
                        eng.wait_ge(s_vb, b + 1)
                    if past:
                        eng.wait_ge(s_w, g0 + j - 1)
                    eng.wait_ge(s_hi, g0 + j + 2)
                    eng.wait_ge(s_lo, g0 + j + 2)
                    tile = "first" if head and j == 0 else "mid"
                    conv(g0 + j, j, 0, tile, range(3))
                    product_b(g0 + j + 2, (j + 2) % 4, 0, b + 1 if tail and j == 2 else None)
                    conv(g0 + j, j, 0, tile, range(3, TAPS))
                    if not first and head and j == 2:
                        layer1_mean(b - 1)
                    if tail and j == 1:
                        kernels(b + 1)
                    if tail and j == 2:
                        spread(b + 1, 0)
                    if past:
                        product_out(out_n, 1)
                    product_b(g0 + j + 2, (j + 2) % 4, 1, None)
                    if l1:
                        layer1(4 * (Q + off) + k, k, far if off == -5 else near, 1, None)
                    if tail and j == 0:
                        pooled_products(b + 1)
                    if tail and j == 2:
                        spread(b + 1, 1)
                    tile = "last" if tail and j == 3 else "mid"
                    conv(g0 + j, j, 1, tile, range(6))
                    product_side(g0 + j + 2, (j + 2) % 4)
                    conv(g0 + j, j, 1, tile, range(6, TAPS), True)

            def epilogue():
                n = B * STRIPS
                for m in range(n - STRIPS - 3, n - STRIPS):
                    for t in range(2):
                        layer1(m, m % 4, slot(m // 4, 0), t, None)
                for k in (n - 2, n - 1):
                    for t in range(2):
                        product_out(k, t)
                group_moments("1", B - 1)
                layer1_mean(B - 1)
                for s in range(STRIPS):
                    for t in range(2):
                        m = n - STRIPS + s
                        layer1(m, s % 4, slot(m // 4, 0), t, B if s == 0 and t == 0 else None, last_bank(s, t), 4)

            image_loop(eng, prologue, quad, epilogue)

        @block.vector
        def _(eng):
            V = nc.vector

            def moments_0():
                agg = st["x"]["agg"]
                eng.wait_ge(s_b0, 2 * STRIPS)
                V.bn_aggr(agg[:], bnx).then_inc(hk["xagg"], 1)
                eng.wait_ge(hk["xagg"], 1)
                V.scalar_tensor_tensor(out=agg[:, 1:2], in0=agg[:, 0:1], scalar=agg[:, 0:1],
                                       in1=agg[:, 1:2], op0=ALU.mult, op1=ALU.add).then_inc(hk["xmom"], 1)

            def tap_matrices(i, u):
                eng.wait_ge(s_wn, i + 1)
                eng.wait_ge(s_kbc, 3 * i + u + 1)
                if not isinstance(i, int) or i > 0 or u > 0:
                    eng.wait_ge(s_wsl, 3 * i + u)
                V.tensor_tensor(wtmp[:].rearrange("p (k o) -> p k o", o=C),
                                psM[:, 0:3 * C].rearrange("p (k o) -> p k o", o=C),
                                wn[:, None, 0:C].broadcast_to([C, 3, C]), ALU.mult).then_inc(s_wt, 1)

            def switch_a(i, done):
                eng.wait_ge(s_wsh, 3 * i + 3)
                eng.wait_ge(s_wsl, 3 * i + 3)
                if done is not None:
                    eng.wait_ge(s_cv, done)
                V.tensor_copy(wa[:, 0, :], wst[:, 0, :]).then_inc(s_wa, 1)
                V.tensor_copy(wa[:, 1, :], wst[:, 1, :]).then_inc(s_wa, 1)
                if done is not None:
                    eng.wait_ge(s_tap, done * TAPS)
                    eng.wait_ge(s_st, done * TAPS)
                V.tensor_copy(kb[:], kk[:]).then_inc(s_kb, 1)
                eng.wait_ge(s_kb, i + 1)

            def tap(n, j, k):
                if k == 0:
                    eng.wait_ge(s_xe, 3 * n + 4)
                    if not isinstance(n, int) or n >= 2:
                        eng.wait_ge(s_w, n - 1)
                else:
                    eng.wait_ge(s_tap, n * TAPS + k)
                dy, dx = k // 3, k % 3
                src = xh[:, 8 * j + dy:8 * j + dy + 8, dx:dx + W]
                dst = acc[:, j % 2, :].rearrange("p (r c) -> p r c", c=W)
                if k == 0:
                    V.tensor_scalar(dst, src, kb[:, TAPS:TAPS + 1], None, ALU.mult).then_inc(s_tap, 1)
                else:
                    V.scalar_tensor_tensor(out=dst, in0=src, scalar=kb[:, TAPS + k:TAPS + k + 1], in1=dst,
                                           op0=ALU.mult, op1=ALU.add).then_inc(s_tap, 1)

            def side_tap(n, j, k):
                if k == 0:
                    eng.wait_ge(s_xe, 3 * n + 6)
                    if not isinstance(n, int) or n >= 1:
                        eng.wait_ge(s_st, n * TAPS)
                else:
                    eng.wait_ge(s_st, n * TAPS + k)
                dy, dx = k // 3, k % 3
                src = side[:, 8 * j + dy:8 * j + dy + 8, dx:dx + SIDE]
                if k == 0:
                    V.tensor_scalar(sacc[:], src, kb[:, 0:1], None, ALU.mult).then_inc(s_st, 1)
                    return
                dst = sacc[:]
                if k == TAPS - 1:
                    eng.wait_ge(s_cv, n + 1)
                    dst = psA[:, j % 2, :].rearrange("p (r c) -> p r c", c=W)[:, :, 0:SIDE]
                V.scalar_tensor_tensor(out=dst, in0=src, scalar=kb[:, k:k + 1], in1=sacc[:],
                                       op0=ALU.mult, op1=ALU.add).then_inc(s_st, 1)

            def bound(n):
                eng.wait_ge(s_exp, n + 1)
                V.tensor_scalar(em[:], em[:], EMAX, None, ALU.min).then_inc(s_cl, 1)

            def weigh(n, par, h):
                if h == 0:
                    eng.wait_ge(s_act, 3 * n + 3)
                    if not isinstance(n, int) or n >= 1:
                        eng.wait_ge(s_om, 2 * n)
                y = psA[:, par, :] if h == 0 else acc[:, par, :]
                last = V.scalar_tensor_tensor(out=wm[:, h * SP:(h + 1) * SP], in0=em[:, h * SP:(h + 1) * SP],
                                              scalar=0.5, in1=y, op0=ALU.subtract, op1=ALU.mult)
                if h == 1:
                    last.then_inc(s_w, 1)

            def residual(n, k, base, t, s, i=None):
                eng.wait_ge(s_om, 2 * n + t + 1)
                if i is not None:
                    eng.wait_ge(hk["1mom"], i)
                xs = X[:, bass.ds(base + k * SP + t * TP, TP)]
                V.scalar_tensor_tensor(out=xs, in0=psO[:], scalar=boutp[:, 0:1], in1=xs, op0=ALU.add,
                                       op1=ALU.add, accum_out=sum1[:, bass.ds(2 * s + t, 1)]).then_inc(s_x1, 1)

            def prologue():
                V.memset(hi[:], 0.0).then_inc(s_zero, 1)
                V.memset(lo[:], 0.0).then_inc(s_zero, 1)
                V.memset(xh[:], 0.0).then_inc(s_zero, 1)
                V.memset(zrow[:], 0.0).then_inc(s_zero, 1)
                V.memset(bx[:], 0.0).then_inc(s_zero, 1)
                V.memset(hv[:], 0.0).then_inc(s_zero, 1)
                V.memset(side[:], 0.0).then_inc(s_zero, 1)
                for c in range(2 * STRIPS):
                    if c % 2 == 0:
                        eng.wait_ge(s_first[c // 2], 16)
                    V.bn_stats(bnx[:, c, :], X[:, c * TP:(c + 1) * TP]).then_inc(s_b0, 1)
                moments_0()
                eng.wait_ge(s_const, 16 * len(consts))
                eng.wait_ge(s_w2, 1)
                V.tensor_tensor(w2p[:, 1], w2t, w2p[:, 0], ALU.subtract).then_inc(s_w2, 1)
                for u in range(3):
                    tap_matrices(0, u)

            def quad(b, q, Q, era, kind):
                first = era == 0
                g0 = snap(eng, Q * 4)
                cur = snap(eng, slot(Q, 0))
                prev = snap(eng, slot(Q, -1))
                head, tail = kind == "head", kind == "tail"
                for j in range(4):
                    n = g0 + j
                    s1 = j - 2 + (STRIPS if head and j < 2 else q * 4)
                    base1 = cur if j >= 2 else prev
                    k1 = (j - 2) % 4
                    out_on = not (first and head and j < 2)
                    mish_on = not (first and head and j == 0)

                    def late(t):
                        if out_on:
                            fresh = head and j == 2 and t == 0 and not first
                            residual(n - 2, k1, base1, t, s1, b if fresh else None)

                    if mish_on:
                        side_tap(n - 1, (j - 1) % 4, TAPS - 1)
                    if head and j == 0:
                        switch_a(b, None if first else g0)
                    tap(n, j, 0)
                    side_tap(n, j, 0)
                    tap(n, j, 1)
                    late(0)
                    if mish_on:
                        bound(n - 1)
                    for k in range(1, 6):
                        side_tap(n, j, k)
                        tap(n, j, k + 1)
                        if tail and j == 2 and k == 4:
                            tap_matrices(b + 1, 0)
                        if tail and j == 3 and k == 4:
                            tap_matrices(b + 1, 2)
                    side_tap(n, j, 6)
                    if mish_on:
                        weigh(n - 1, (j - 1) % 2, 0)
                    tap(n, j, 7)
                    side_tap(n, j, 7)
                    if mish_on:
                        weigh(n - 1, (j - 1) % 2, 1)
                    late(1)
                    tap(n, j, 8)
                    if tail and j == 2:
                        tap_matrices(b + 1, 1)

            def epilogue():
                n = B * STRIPS
                side_tap(n - 1, 3, TAPS - 1)
                bound(n - 1)
                for t in range(2):
                    residual(n - 2, 2, slot((n - 2) // 4, 0), t, STRIPS - 2)
                weigh(n - 1, 1, 0)
                weigh(n - 1, 1, 1)
                for t in range(2):
                    residual(n - 1, 3, slot((n - 1) // 4, 0), t, STRIPS - 1)
                for m in range(n - STRIPS, n):
                    for t in range(2):
                        eng.wait_ge(s_re, 2 * m + t + 1 + FREE)
                        at = slot(m // 4, 0) + (m % 4) * SP + t * TP
                        V.tensor_tensor(X[:, at:at + TP], X[:, at:at + TP], zt[:, t, :], ALU.add).then_inc(s_add, 1)

            image_loop(eng, prologue, quad, epilogue)

        @block.gpsimd
        def _(eng):
            P = nc.gpsimd
            def variance(who, i, s):
                d = st[who]
                eng.wait_ge(hk[who + "gsb"], i + 1)
                P.tensor_tensor(d["t"][:], d["gm"][:, 0:1], d["gm"][:, 0:1], ALU.mult).then_inc(s, 1)
                eng.wait_ge(s, 7 * i + 1)
                P.tensor_tensor(d["t"][:], d["gm"][:, 1:2], d["t"][:], ALU.subtract).then_inc(s, 1)
                eng.wait_ge(s, 7 * i + 2)
                apart(eng)
                P.tensor_scalar(d["v"][:], d["t"][:], EPS, None, ALU.add).then_inc(hk[who + "var"], 1)

            def rstd(who, i, s):
                d = st[who]
                eng.wait_ge(hk[who + "r0"], i + 1)
                P.tensor_tensor(d["t"][:], d["r0"][:], d["r0"][:], ALU.mult).then_inc(s, 1)
                eng.wait_ge(s, 7 * i + 3)
                P.tensor_tensor(d["t"][:], d["t"][:], d["v"][:], ALU.mult).then_inc(s, 1)
                eng.wait_ge(s, 7 * i + 4)
                apart(eng)
                P.tensor_scalar(d["t"][:], d["t"][:], -0.5, 1.5, ALU.mult, ALU.add).then_inc(s, 1)
                eng.wait_ge(s, 7 * i + 5)
                P.tensor_tensor(d["r"][:], d["r0"][:], d["t"][:], ALU.mult).then_inc(s, 1)
                P.tensor_tensor(d["mm"][:, 0:1], d["agg"][:, 0:1], d["gm"][:, 0:1], ALU.subtract).then_inc(hk[who + "pool"], 1)
                eng.wait_ge(s, 7 * i + 6)
                eng.wait_ge(hk[who + "pool"], i + 1 + (who == "1"))
                P.tensor_tensor(d["mm"][:, 0:1], d["mm"][:, 0:1], d["r"][:], ALU.mult).then_inc(s, 1)
                P.tensor_tensor(d["mm"][:, 1:2], d["gm"][:, 0:1], d["r"][:], ALU.mult).then_inc(hk[who + "r"], 1)
                eng.wait_ge(s, 7 * i + 7)
                eng.wait_ge(hk[who + "r"], i + 1)

            def fold(i):
                if not isinstance(i, int) or i > 0:
                    eng.wait_ge(s_wt, 3 * i)
                apart(eng)
                P.tensor_scalar(wn[:], wint[:], st["x"]["r"][:, 0:1], None, ALU.mult).then_inc(s_wn, 1)

            def pool_bias(i):
                pv = pm[:].rearrange("p (h a) -> p a h", a=2)
                eng.wait_ge(s_psb, i + 1)
                P.tensor_tensor(pooled[:], pv[:, 0, :], binp[:], ALU.add)
                P.tensor_tensor(bp[:], binp[:], pv[:, 1, :], ALU.subtract).then_inc(s_pl, 1)

            def hidden_low(i):
                eng.wait_ge(s_hvh, i + 1)
                P.tensor_tensor(hv[:, :, 0], hcx[:], hv[:, :, 1], ALU.subtract).then_inc(s_hvl, 1)

            def kernel_bias(i):
                eng.wait_ge(s_ksb, i + 1)
                kv = kraw[:].rearrange("p (k a) -> p a k", a=2)
                P.tensor_tensor(kk[:], kv[:, 0, :], kv[:, 1, :], ALU.add).then_inc(s_ks, 1)
                eng.wait_ge(s_ks, i + 1)
                P.tensor_tensor(kk[:], kk[:], b2p[:], ALU.add).then_inc(s_kk, 1)
                eng.wait_ge(s_kk, i + 1)
                eng.wait_ge(s_pl, i + 1)
                apart(eng)
                P.tensor_scalar(bk[:], kk[:, 0:TAPS], bp[:, 0:1], None, ALU.mult).then_inc(s_bst, 1)
                eng.wait_ge(s_bst, 2 * i + 1)
                apart(eng)
                P.tensor_copy(bh[:], bk[:]).then_inc(s_bst, 1)
                eng.wait_ge(s_bst, 2 * i + 2)
                apart(eng)
                P.tensor_copy(bx[:, 0:TAPS], bh[:])
                P.tensor_tensor(bx[:, 32:32 + TAPS], bk[:], bh[:], ALU.subtract).then_inc(s_bxr, 1)

            def taps_low(i, u):
                eng.wait_ge(s_wsh, 3 * i + u + 1)
                part = slice(3 * u * C, 3 * (u + 1) * C)
                P.tensor_tensor(wst[:, 1, part], wtmp[:], wst[:, 0, part], ALU.subtract).then_inc(s_wsl, 1)

            def switch_b(i):
                eng.wait_ge(s_wbh, i + 1)
                eng.wait_ge(s_wn, i + 1)
                P.tensor_tensor(wb[:, 1, :], wn[:], wb[:, 0, :], ALU.subtract).then_inc(s_wbl, 1)

            def fold_1(i, done):
                eng.wait_ge(s_re, done)
                apart(eng)
                P.tensor_scalar(lpt[:], lt[:], st["1"]["r"][:, 0:1], None, ALU.mult).then_inc(s_lpt, 1)

            def cast(n, j, base, row):
                eng.wait_ge(s_hi, n + 1)
                xs = X[:, bass.ds(base + j * SP, SP)].rearrange("p (r c) -> p r c", c=W)
                apart(eng)
                if row == "top":
                    P.memset(lo[:, 0, :], 0.0)
                elif row == "bottom":
                    P.memset(lo[:, RING + 1, :], 0.0)
                elif j in (0, 3):
                    p, r = (RING + 1, 0) if j == 0 else (0, ROWS - 1)
                    P.tensor_tensor(lo[:, p, 1:1 + W], xs[:, r, :], hi[:, p, 1:1 + W], ALU.subtract)
                P.tensor_tensor(lo[:, 8 * j + 1:8 * j + 9, 1:1 + W], xs,
                                hi[:, 8 * j + 1:8 * j + 9, 1:1 + W], ALU.subtract).then_inc(s_lo, 1)

            def add(n, k, base, t):
                eng.wait_ge(s_re, 2 * n + t + 1 + FREE)
                xs = X[:, bass.ds(base + k * SP + t * TP, TP)]
                P.tensor_tensor(xs, xs, zt[:, t, :], ALU.add).then_inc(s_add, 1)

            s_px, s_p1 = s_chain["x"], s_chain["1"]

            def prologue():
                eng.wait_ge(s_const, 16 * len(consts))
                eng.wait_ge(s_zero, 7)
                for t in range(FREE):
                    P.memset(bk[:], 0.0).then_inc(s_add, 1)
                    eng.wait_ge(s_add, t + 1)
                P.memset(bk[:], 0.0).then_inc(hk["1pool"], 1)
                eng.wait_ge(hk["1pool"], 1)
                variance("x", 0, s_px)
                rstd("x", 0, s_px)
                fold(0)
                pool_bias(0)
                switch_b(0)
                hidden_low(0)
                kernel_bias(0)
                for u in range(3):
                    taps_low(0, u)
                for n in range(2):
                    cast(n, n, 0, "top" if n == 0 else None)

            def quad(b, q, Q, era, kind):
                g0 = snap(eng, Q * 4)
                cur = snap(eng, slot(Q, 0))
                nxt = snap(eng, slot(Q, 1))
                near = snap(eng, slot(Q, -4))
                first = era == 0
                head, tail = kind == "head", kind == "tail"
                for j in range(4):
                    row = "bottom" if tail and j == 1 else "top" if tail and j == 2 else None
                    cast(g0 + j + 2, (j + 2) % 4, cur if j < 2 else nxt, row)
                    if tail and j == 1:
                        hidden_low(b + 1)
                    if tail and j == 2:
                        switch_b(b + 1)
                    if tail and j == 0:
                        variance("x", b + 1, s_px)
                        rstd("x", b + 1, s_px)
                        fold(b + 1)
                    if not first and head and j == 2:
                        variance("1", b - 1, s_p1)
                        rstd("1", b - 1, s_p1)
                    if tail and j == 3:
                        taps_low(b + 1, 1)
                    l1 = l1_strip(j, kind, era)
                    for t in range(2):
                        if l1:
                            off, k = l1
                            add(4 * (Q + off) + k, k, nxt if off == -5 else near, t)
                        if tail and j == 2 and t == 0:
                            taps_low(b + 1, 0)
                        if tail and j == 3 and t == 0:
                            taps_low(b + 1, 2)
                    if not first and head and j == 2:
                        fold_1(b - 1, 2 * (g0 - STRIPS) + FREE)
                    if tail and j == 0:
                        pool_bias(b + 1)
                    if tail and j == 1:
                        kernel_bias(b + 1)

            def epilogue():
                n = B * STRIPS
                for m in range(n - STRIPS - 3, n - STRIPS):
                    for t in range(2):
                        add(m, m % 4, slot(m // 4, 0), t)
                variance("1", B - 1, s_p1)
                rstd("1", B - 1, s_p1)
                fold_1(B - 1, 2 * (n - STRIPS) + FREE)

            image_loop(eng, prologue, quad, epilogue)


def _layout(inputs):
    import numpy as np
    n = lambda k: np.asarray(inputs[k])
    halves = lambda v: np.ascontiguousarray(v.reshape(2, C).T)
    k_in = lambda m: np.ascontiguousarray(m.reshape(2, C, -1).transpose(1, 0, 2))
    a = {}
    a["x"] = n("x").reshape(B, C, H * W)
    a["w_in_t"] = np.ascontiguousarray(n("L0_conv_w_in").T)
    a["b_in"] = halves(n("L0_conv_b_in"))
    a["w1_t"] = k_in(n("L0_conv_kg_w1").T)
    a["b1"] = halves(n("L0_conv_kg_b1"))
    w2 = n("L0_conv_kg_w2").reshape(HID, TAPS, HID).transpose(2, 1, 0)
    a["w2_t"] = np.ascontiguousarray(w2.reshape(2, C, TAPS, HID).transpose(1, 0, 2, 3))
    a["b2"] = np.ascontiguousarray(n("L0_conv_kg_b2").reshape(2, C, TAPS).transpose(1, 0, 2).reshape(C, 2 * TAPS))
    a["w_out_t"] = k_in(n("L0_conv_w_out").T)
    a["b_out"] = n("L0_conv_b_out").reshape(C, 1)
    a["mask"] = n("L1_conv_freq_mask").reshape(C, 1)
    a["amp_w"] = n("L1_conv_amp_w")
    a["amp_b"] = n("L1_conv_amp_b").reshape(C, 1)
    a["ph_w"] = n("L1_conv_phase_w")
    a["ph_b"] = n("L1_conv_phase_b").reshape(C, 1)
    f = (np.arange(C) + C // 2) % C
    angle = 2 * np.pi * (f[:, None] * np.arange(C)[None, :] % C) / C
    a["cos_m"] = np.cos(angle).astype(np.float32)
    a["sin_m"] = np.sin(angle).astype(np.float32)
    g = np.arange(C) // GROUP
    a["group_m"] = ((g[:, None] == g[None, :]) / GROUP).astype(np.float32)
    a["ident_m"] = np.eye(C, dtype=np.float32)
    v = np.zeros((64, 6, W), np.float16)
    for tap in range(TAPS):
        dy, dx = tap // 3, tap % 3
        m = np.ones((6, W))
        if dy == 0:
            m[0] = 0
        if dy == 2:
            m[5] = 0
        if dx == 0:
            m[:, 0] = 0
        if dx == 2:
            m[:, W - 1] = 0
        v[tap] = v[32 + tap] = m
    a["valid_m"] = v
    return a


def kernel(**inputs):
    import numpy as _np
    import concourse.bacc as _bacc
    from concourse.bass_utils import run_bass_kernel_spmd as _run

    nc = _bacc.Bacc("TRN2", target_bir_lowering=False, num_devices=1)
    arrays, args = {}, {}
    for name, a in _layout(inputs).items():
        arrays[f"in_{name}_dram"] = a
        args[name] = nc.dram_tensor(f"in_{name}_dram", a.shape, mybir.dt.from_np(a.dtype), kind="ExternalInput").ap()
    out = nc.dram_tensor("out_0_dram", (B, C, H * W), F32, kind="ExternalOutput").ap()
    conv_preact_kernel(nc, out=out, **args)
    r = _run(nc, [arrays], core_ids=[0])
    return r.results[0]["out_0_dram"].reshape(B, C, H, W)
```

```python
import concourse.bass as bass
from concourse import mybir
from contextlib import ExitStack

F32 = mybir.dt.float32
F16 = mybir.dt.float16
ALU = mybir.AluOpType
ACT = mybir.ActivationFunctionType

B, C, H, W = 16, 128, 128, 128
HID = 2 * C
TAPS = 9
ROWS = 8
SP = ROWS * W
TP = SP // 2
STRIPS = H // ROWS
QUADS = STRIPS // 4
PW = W + 2
RING = 32
XG = 6
AHEAD = 4
SIDE = 21
STAT = 20
LOADED = STAT + 1
GROUP = 4
EPS = 1e-5
YMAX = 10.0


def conv_preact_kernel(nc, x, w_in_t, b_in, w1_t, b1, w2_t, b2, w_out_t, b_out, mask, amp_w, amp_b,
                       ph_w, ph_b, cos_m, sin_m, group_m, ident_m, valid_m, out):
    ctx = ExitStack()
    with ctx:
        def sb(name, shape, dt=F32):
            return ctx.enter_context(nc.sbuf_tensor(name, shape, dt))

        def pb(name, shape):
            return ctx.enter_context(nc.psum_tensor(name, shape, F32))

        def sem(name):
            return ctx.enter_context(nc.semaphore(name))

        vectors = sb("vectors", [C, 238])
        taken = [0]

        def few(n):
            taken[0] += n
            return vectors[:, taken[0] - n:taken[0]]

        X = sb("X", [C, XG * 4 * SP])
        XS = sb("XS", [C, SP])
        hi = sb("hi", [C, RING + 2, PW], F16)
        lo = sb("lo", [C, RING + 2, PW], F16)
        xh = sb("xh", [C, RING + 2, PW])
        acc = sb("acc", [C, 2, SP])
        side = sb("side", [C, RING + 2, SIDE + 2])
        sacc = sb("sacc", [C, ROWS, SIDE])
        junk = sb("junk", [C, SP], F16)
        em = sb("em", [C, 2 * SP])
        wm = sb("wm", [C, 2 * SP])
        zt = sb("zt", [C, 2, TP])
        w2p = sb("w2p", [C, 2, 2, TAPS, HID], F16)
        w1t = sb("w1t", [C, 2, HID])
        wint = sb("wint", [C, HID])
        wn = sb("wn", [C, HID])
        woutt = sb("woutt", [C, 2, C])
        ident = sb("ident", [C, C])
        groupm = sb("groupm", [C, C])
        lt = sb("lt", [C, C])
        lpt = sb("lpt", [C, C])
        valid = sb("valid", [64, 6, W - SIDE], F16)
        wa = sb("wa", [C, 2, 2, TAPS * C], F16)
        wtmp = sb("wtmp", [C, 3 * C])
        wb = sb("wb", [C, 2, HID], F16)
        vbst = sb("vbst", [64, C], F16)
        vb = sb("vb", [64, C], F16)
        bx = sb("bx", [C, 64])
        bh = sb("bh", [C, TAPS], F16)
        hv = sb("hv", [C, 2, 4], F16)
        bk = few(TAPS)
        zero = few(1)
        binp = few(2)
        b1p = few(2)
        b2p = few(2 * TAPS)
        boutp = few(1)
        spare = few(4)
        cl = few(1)
        ymax = few(1)
        lb = few(1)
        bpl = few(2)
        sumx, sqx = few(STRIPS), few(STRIPS)
        sum1, sq1 = few(2 * STRIPS), few(STRIPS)
        kk = few(2 * TAPS)
        kb = few(2 * TAPS)
        pooled = few(2)
        bp = few(2)
        pm = few(4)
        hcx = few(2)
        kraw = few(4 * TAPS)
        st = {}
        for who in ("x", "1"):
            st[who] = {k: few(n) for k, n in
                       (("agg", 2), ("gm", 2), ("t", 1), ("v", 1), ("ln", 1), ("r0", 1), ("r", 1), ("mm", 2))}

        bnx = wm[:, 0:12 * STRIPS].rearrange("p (t s) -> p t s", s=6)
        w2t = X[:, STRIPS * SP:STRIPS * SP + 2 * TAPS * HID].rearrange("p (k t o) -> p k t o", k=2, t=TAPS)
        cosm, sinm, ampw, phw = (em[:, i * C:(i + 1) * C] for i in range(4))
        m1 = em[:, 4 * C:6 * C]
        small = em[:, 6 * C:6 * C + 4]
        maskp, ampb, phb, nphb = (small[:, i:i + 1] for i in range(4))

        psA = pb("psA", [C, 2, SP])
        psB = pb("psB", [C, TP])
        psO = pb("psO", [C, TP])
        psL = pb("psL", [C, TP])
        psM = pb("psM", [C, TP])

        s_const = sem("s_const")
        s_xin = [sem(f"s_xin{j}") for j in range(4)]
        s_first = [sem(f"s_first{n}") for n in range(STRIPS)]
        s_sin = sem("s_sin")
        s_out = [sem(f"s_out{j}") for j in range(4)]
        s_zero = sem("s_zero")
        s_hi = sem("s_hi")
        s_lo = sem("s_lo")
        s_xm = sem("s_xm")
        s_xe = sem("s_xe")
        s_cv = sem("s_cv")
        s_tap = sem("s_tap")
        s_st = sem("s_st")
        s_gap = sem("s_gap")
        s_act = sem("s_act")
        s_w = sem("s_w")
        s_om = sem("s_om")
        s_x1 = sem("s_x1")
        s_lm = sem("s_lm")
        s_re = sem("s_re")
        s_add = sem("s_add")
        s_b0 = sem("s_b0")
        s_sx = sem("s_sx")
        s_bx = sem("s_bx")
        s_b1 = sem("s_b1")
        hk = {}
        for who in ("x", "1"):
            for k in ("agg", "mom", "gps", "gsb", "var", "ln", "r0", "r", "pool"):
                hk[who + k] = sem(f"s_{who}_{k}")
        s_wn = sem("s_wn")
        s_pps = sem("s_pps")
        s_psb = sem("s_psb")
        s_pl = sem("s_pl")
        s_hps = sem("s_hps")
        s_hcx = sem("s_hcx")
        s_hvh = sem("s_hvh")
        s_hvl = sem("s_hvl")
        s_ks = sem("s_ks")
        s_w2in = [sem(f"s_w2in{k}") for k in range(2)]
        s_w2h = sem("s_w2h")
        s_w2l = sem("s_w2l")
        s_kps = sem("s_kps")
        s_ksb = sem("s_ksb")
        s_kk = sem("s_kk")
        s_bxr = sem("s_bxr")
        s_bst = sem("s_bst")
        s_tps = sem("s_tps")
        s_vst = sem("s_vst")
        s_kbc = sem("s_kbc")
        s_wt = sem("s_wt")
        s_wsh = sem("s_wsh")
        s_wsl = sem("s_wsl")
        s_vb = sem("s_vb")
        s_kb = sem("s_kb")
        s_wbh = sem("s_wbh")
        s_wbl = sem("s_wbl")
        s_bpl = sem("s_bpl")
        s_lps = sem("s_lps")
        s_lpt = sem("s_lpt")
        s_lb = sem("s_lb")
        s_i = sem("s_i")
        s_j = sem("s_j")
        s_chain = {who: sem(f"s_chain_{who}") for who in ("x", "1")}

        s_apart = sem("s_apart")

        consts = [
            (cosm, cos_m), (sinm, sin_m), (ampw, amp_w), (phw, ph_w), (maskp, mask), (ampb, amp_b),
            (phb, ph_b), (groupm[:], group_m), (ident[:], ident_m), (valid[:], valid_m), (wint[:], w_in_t),
            (binp[:], b_in), (b1p[:], b1), (b2p[:], b2), (boutp[:], b_out), (w1t[:], w1_t),
            (woutt[:], w_out_t),
        ]

        block = ctx.enter_context(nc.Block())

        FREE = 2

        def snap(eng, v):
            return v if isinstance(v, int) else eng.snap(v)

        def apart(eng):
            eng.sem_inc(s_apart, 1)

        def last_bank(s, t):
            return psA[:, s % 2, t * TP:(t + 1) * TP]

        def early_bank(n, t):
            return ((psB[:], psO[:]), (psL[:], last_bank(1, 0)))[n][t]

        def early_side(n):
            return last_bank(1, 1)[:, n * TP // 2:n * TP // 2 + ROWS * (SIDE + 1)]

        def spill_bank(m, t):
            return (psL[:], last_bank(0, 0), last_bank(0, 1))[(2 * (m - (B - 1) * STRIPS + 3) + t) % 3]

        def slot(Q, k):
            return ((Q + (k % XG)) % XG) * (4 * SP)

        def image_loop(eng, prologue, quad, epilogue):
            prologue()
            for era in range(3):
                def image(b, par):
                    quad(b, 0, b * QUADS, era, "head", par)
                    with eng.Fori(1, QUADS - 1) as q:
                        quad(b, q, b * QUADS + q, era, "mid", par)
                    quad(b, QUADS - 1, b * QUADS + QUADS - 1, era, "tail", par)
                if era < 2:
                    image(era, era)
                else:
                    with eng.Fori(1, B // 2) as pair:
                        for par in range(2):
                            image(pair * 2 + par, par)
            epilogue()

        def l1_strip(j, kind, era):
            if era == 0 or (era == 1 and kind == "head" and j < 3):
                return None
            return (-5, j + 1) if j < 3 else (-4, 0)

        @block.sync
        def _(eng):
            xr = x.rearrange("b c n -> c b n")
            outr = out.rearrange("b c n -> c b n")

            def load_x(n4, j, b, px, base, free, used):
                if free is not None:
                    eng.wait_ge(s_out[j], free)
                    apart(eng)
                if used is not None:
                    eng.wait_ge(s_hi, used)
                apart(eng)
                eng.dma_start(X[:, bass.ds(base + j * SP, SP)], xr[:, bass.ds(b, 1), bass.ds(px, SP)]
                              .rearrange("c b n -> c (b n)")).then_inc(s_xin[j], 16)

            def load_stat(b, px, used):
                if used is not None:
                    eng.wait_ge(s_bx, used)
                apart(eng)
                eng.dma_start(XS[:], xr[:, bass.ds(b, 1), bass.ds(px, SP)]
                              .rearrange("c b n -> c (b n)")).then_inc(s_sin, 16)

            def store(k, j, b, px, base, n):
                eng.wait_ge(s_add, 2 * n + 2 + FREE)
                apart(eng)
                eng.wait_ge(s_out[j], 16 * (k + 1))
                apart(eng)
                eng.dma_start(outr[:, bass.ds(b, 1), bass.ds(px, SP)].rearrange("c b n -> c (b n)"),
                              X[:, bass.ds(base + j * SP, SP)]).then_inc(s_out[j], 16)

            def constants():
                for j in range(4):
                    eng.dma_start(spare[:, j:j + 1], b_out).then_inc(s_out[j], 16)
                for dst, src in consts:
                    eng.dma_start(dst, src).then_inc(s_const, 16)

            def prologue():
                for n in range(STRIPS):
                    eng.dma_start(X[:, n * SP:(n + 1) * SP], xr[:, 0, n * SP:(n + 1) * SP]).then_inc(s_first[n], 16)
                    if n == 1:
                        constants()
                for k in range(2):
                    eng.dma_start(w2t[:, k], w2_t[:, k]).then_inc(s_w2in[k], 16)
                load_stat(1, 0, None)

            def quad(b, q, Q, era, kind, par):
                first = era == 0
                g0 = snap(eng, Q * 4)
                nxt = snap(eng, slot(Q, 1))
                old = snap(eng, slot(Q, -4))
                bl = snap(eng, (b + (1 if kind == "tail" else 0)) % B)
                ql = 0 if kind == "tail" else q + 1
                for j in range(4):
                    l1 = l1_strip(j, kind, era)
                    if l1:
                        off, k = l1
                        before = kind == "head" and off == -5
                        qq = q + off + QUADS * (2 if before else 1)
                        store(Q + off, k, b - (2 if before else 1), (qq * 4 + k) * SP,
                              nxt if off == -5 else old, (Q + off) * 4 + k)
                    if not (first and kind != "tail"):
                        load_x(Q + 1, j, bl, (ql * 4 + j) * SP, nxt, None if first else 16 * (Q - 3), g0 + j + 1)
                    if first and kind == "head":
                        for m in (2 * j + 1, 2 * j + 2):
                            load_stat(1, m * SP, m)
                    else:
                        ns = snap(eng, g0 + j + LOADED)
                        load_stat((ns // STRIPS) % B, (ns % STRIPS) * SP, ns - STRIPS)

            def epilogue():
                for n in range(B * STRIPS - STRIPS - 3, B * STRIPS):
                    store(n // 4, n % 4, n // STRIPS, n % STRIPS * SP, slot(n // 4, 0), n)
                for j in range(4):
                    eng.wait_ge(s_out[j], 16 * (B * QUADS + 1))

            image_loop(eng, prologue, quad, epilogue)
            for j in range(4):
                eng.wait_ge(s_xin[j], 16 * (B * QUADS + 1 - QUADS))
            eng.wait_ge(s_sin, 16 * (B * STRIPS + LOADED - STRIPS))

        @block.scalar
        def _(eng):
            act = nc.scalar.activation

            def stats_group(who, i):
                eng.wait_ge(hk[who + "gps"], i + 1)
                act(st[who]["gm"][:], psM[:, 0:2], ACT.Copy).then_inc(hk[who + "gsb"], 1)

            def stats_rstd(who, i):
                d = st[who]
                eng.wait_ge(hk[who + "var"], i + 1)
                act(d["ln"][:], d["v"][:], ACT.Ln).then_inc(hk[who + "ln"], 1)
                eng.wait_ge(hk[who + "ln"], i + 1)
                act(d["r0"][:], d["ln"][:], ACT.Exp, scale=-0.5).then_inc(hk[who + "r0"], 1)

            def pooled_out(i):
                eng.wait_ge(s_pps, i + 1)
                act(pm[:], psM[:, 0:4], ACT.Copy).then_inc(s_psb, 1)

            def hidden_out(i):
                eng.wait_ge(s_hps, i + 1)
                for h in range(2):
                    last = act(hcx[:, h:h + 1], psM[:, h:h + 1], ACT.Relu, bias=b1p[:, h:h + 1])
                last.then_inc(s_hcx, 1)
                eng.wait_ge(s_hcx, i + 1)
                act(hv[:, :, 1], hcx[:], ACT.Copy).then_inc(s_hvh, 1)

            def kernels_out(i):
                eng.wait_ge(s_kps, i + 1)
                act(kraw[:], psM[:, 0:4 * TAPS], ACT.Copy).then_inc(s_ksb, 1)

            def bias_out(i):
                eng.wait_ge(s_tps, i + 1)
                act(vbst[:], psM[0:64, 0:C], ACT.Copy).then_inc(s_vst, 1)

            def taps_high(i, u, par):
                eng.wait_ge(s_wt, 3 * i + u + 1)
                act(wa[:, par, 0, 3 * u * C:3 * (u + 1) * C], wtmp[:], ACT.Copy).then_inc(s_wsh, 1)

            def switch_b(i, done):
                if done is not None:
                    eng.wait_ge(s_xm, done)
                eng.wait_ge(s_wn, i + 1)
                act(wb[:, 0, :], wn[:], ACT.Copy).then_inc(s_wbh, 1)
                if done is not None:
                    eng.wait_ge(s_xe, done)
                eng.wait_ge(s_pl, i + 1)
                act(bpl[:], bp[:], ACT.Copy).then_inc(s_bpl, 1)

            def switch_a(i, done):
                if done is not None:
                    eng.wait_ge(s_cv, done)
                eng.wait_ge(s_vst, i + 1)
                act(vb[:], vbst[:], ACT.Copy).then_inc(s_vb, 1)

            def cast(n, n4, j, base, row, there):
                if there:
                    eng.wait_ge(s_first[n] if isinstance(n, int) else s_first[STRIPS - 1], 16)
                else:
                    eng.wait_ge(s_xin[j], 16 * (n4 + 1 - QUADS))
                if not isinstance(n, int) or n >= 3:
                    eng.wait_ge(s_cv, n - 2)
                xs = X[:, bass.ds(base + j * SP, SP)].rearrange("p (r c) -> p r c", c=W)
                edge_row(eng, hi, j, row, lambda r: xs[:, r * (ROWS - 1), :])
                act(hi[:, 8 * j + 1:8 * j + 9, 1:1 + W], xs, ACT.Copy).then_inc(s_hi, 1)

            def edge_row(eng, ring, j, row, src, bias=None):
                pw = ring.shape[2]
                if row == "top":
                    act(ring[:, 0, :], zero.broadcast_to([C, pw]), ACT.Copy)
                elif row == "bottom":
                    act(ring[:, RING + 1, :], zero.broadcast_to([C, pw]), ACT.Copy)
                elif j == 0 or j == 3:
                    dst = ring[:, RING + 1 if j == 0 else 0, 1:(1 + W if pw == PW else pw)]
                    r = 0 if j == 0 else 1
                    if bias is None:
                        act(dst, src(r), ACT.Copy)
                    else:
                        act(dst, src(r), ACT.Identity, bias=bias)

            def evacuate(n, j, t, row, i, bank=None):
                eng.wait_ge(s_xm, 3 * n + t + 1)
                if t == 0:
                    if not isinstance(n, int) or n >= 3:
                        eng.wait_ge(s_tap, (n - 2) * TAPS)
                    if row == "top":
                        eng.wait_ge(s_bpl, i + 1)
                ps = (psB[:] if bank is None else bank).rearrange("p (r c) -> p r c", c=W)
                if (j == 0 and t == 0) or (j == 3 and t == 1):
                    edge_row(eng, xh, j, row, lambda r: ps[:, r * 3, :], bias=bpl[:, 1:2])
                r0 = 8 * j + 4 * t + 1
                act(xh[:, r0:r0 + 4, 1:1 + W], ps, ACT.Identity, bias=bpl[:, 1:2]).then_inc(s_xe, 1)

            def evacuate_side(n, j, row, at=None):
                eng.wait_ge(s_xm, 3 * n + 3)
                if not isinstance(n, int) or n >= 3:
                    eng.wait_ge(s_st, (n - 2) * TAPS)
                ps = (psB[:, 0:ROWS * (SIDE + 1)] if at is None else at).rearrange("p (r c) -> p r c", c=SIDE + 1)
                edge_row(eng, side, j, row, lambda r: ps[:, r * (ROWS - 1), :], bias=bpl[:, 0:1])
                act(side[:, 8 * j + 1:8 * j + 9, 1:2 + SIDE], ps, ACT.Identity, bias=bpl[:, 0:1]).then_inc(s_xe, 1)

            def sums_x(s, count, squares):
                eng.wait_ge(s_sin, 16 * count)
                if squares is not None:
                    eng.wait_ge(s_b1, squares)
                elif not isinstance(count, int) or count > 1:
                    eng.wait_ge(s_bx, count - 1)
                act(junk[:], XS[:], ACT.Copy, accum_out=sumx[:, bass.ds(s, 1)]).then_inc(s_sx, 1)
                eng.wait_ge(s_sx, count)
                act(junk[:], XS[:], ACT.Square, accum_out=sqx[:, bass.ds(s, 1)]).then_inc(s_bx, 1)

            def squares_1(n, k, base, s, sums):
                eng.wait_ge(s_x1, 2 * n + 2)
                eng.wait_ge(s_bx, sums)
                act(junk[:], X[:, bass.ds(base + k * SP, SP)], ACT.Square,
                    accum_out=sq1[:, bass.ds(s, 1)]).then_inc(s_b1, 1)

            def moments(who, i, done):
                sums, squares = (sumx, sqx) if who == "x" else (sum1, sq1)
                agg = st[who]["agg"]
                eng.wait_ge(s_bx if who == "x" else s_b1, done)
                eng.wait_ge(hk[who + "pool"], i + (who == "1"))
                act(junk[:, 0:sums.shape[1]], sums[:], ACT.Copy, scale=1.0 / (H * W), accum_out=agg[:, 0:1])
                act(junk[:, 2 * STRIPS:3 * STRIPS], squares[:], ACT.Copy, scale=1.0 / (H * W),
                    accum_out=agg[:, 1:2]).then_inc(hk[who + "mom"], 1)
                eng.wait_ge(hk[who + "mom"], i + 1)

            def mish_gap(n, par):
                if not isinstance(n, int) or n >= 1:
                    eng.wait_ge(s_w, n)
                eng.wait_ge(s_cv, n + 1)
                eng.wait_ge(s_st, (n + 1) * TAPS)
                act(em[:, 0:SP], psA[:, par, :], ACT.Relu, bias=ymax[:, 0:1], scale=-1.0)
                eng.wait_ge(s_tap, (n + 1) * TAPS)
                act(em[:, SP:2 * SP], acc[:, par, :], ACT.Relu, bias=ymax[:, 0:1], scale=-1.0).then_inc(s_gap, 1)

            def mish_exp(n):
                eng.wait_ge(s_gap, n + 1)
                act(em[:], em[:], ACT.Exp, bias=ymax[:, 0:1], scale=-1.0).then_inc(s_act, 1)

            def mish_square(n):
                eng.wait_ge(s_act, 4 * n + 1)
                act(em[:], em[:], ACT.Square, bias=1.0).then_inc(s_act, 1)

            def mish_ln(n):
                eng.wait_ge(s_act, 4 * n + 2)
                act(em[:], em[:], ACT.Ln, bias=1.0).then_inc(s_act, 1)

            def mish_inverse(n):
                eng.wait_ge(s_act, 4 * n + 3)
                act(em[:], em[:], ACT.Exp, scale=-1.0).then_inc(s_act, 1)

            def relu(n, t, i, ps=None):
                if i is not None:
                    eng.wait_ge(s_lb, i)
                eng.wait_ge(s_lm, 2 * n + t + 1)
                eng.wait_ge(s_add, 2 * n + t - 1 + FREE)
                act(zt[:, t, :], psL[:] if ps is None else ps, ACT.Relu, bias=lb[:, 0:1]).then_inc(s_re, 1)

            def layer1_bias(i):
                eng.wait_ge(s_lps, i + 1)
                eng.wait_ge(s_re, 2 * STRIPS * i + FREE)
                act(lb[:], psM[:, 0:1], ACT.Identity, bias=cl[:, 0:1], scale=-1.0).then_inc(s_lb, 1)

            def prologue():
                nc.scalar.preload_act_table_set("natural_log_exp_and_others")
                eng.wait_ge(s_const, 16 * len(consts))
                eng.wait_ge(s_i, 1)
                act(m1[:, 0:C], psM[:, 0:C], ACT.Copy, scale=maskp)
                act(m1[:, C:2 * C], psM[:, C:2 * C], ACT.Copy, scale=maskp)
                act(nphb, phb, ACT.Copy, scale=-1.0).then_inc(s_j, 1)
                eng.wait_ge(s_i, 2)
                act(lt[:], psM[:, 0:C], ACT.Copy, scale=1.0 / C)
                act(cl[:], psM[:, C:C + 1], ACT.Copy, scale=1.0 / C)
                act(woutt[:], woutt[:], ACT.Copy, scale=-2.0).then_inc(s_j, 1)
                eng.wait_ge(s_j, 2)
                eng.wait_ge(s_zero, 8)
                for t in range(FREE):
                    act(zt[:, t, 0:1], zero, ACT.Copy).then_inc(s_re, 1)
                for n in range(2):
                    cast(n, 0, n, 0, "top" if n == 0 else None, True)
                stats_group("x", 0)
                stats_rstd("x", 0)
                pooled_out(0)
                switch_b(0, None)
                hidden_out(0)
                for k in range(2):
                    eng.wait_ge(s_w2in[k], 16)
                    act(w2p[:, 0, k], w2t[:, k], ACT.Copy).then_inc(s_w2h, 1)
                kernels_out(0)
                bias_out(0)
                for u in range(3):
                    taps_high(0, u, 0)
                for n in range(2):
                    row = "top" if n == 0 else None
                    for t in range(2):
                        evacuate(n, n, t, row, 0, early_bank(n, t))
                    evacuate_side(n, n, row, early_side(n))

            def quad(b, q, Q, era, kind, par):
                first = era == 0
                g0 = snap(eng, Q * 4)
                prev = snap(eng, slot(Q, -1))
                cur = snap(eng, slot(Q, 0))
                nxt = snap(eng, slot(Q, 1))
                for j in range(4):
                    head, tail = kind == "head", kind == "tail"
                    if tail and j == 0:
                        moments("x", b + 1, g0 + STAT - STRIPS)
                    if head and j == 0:
                        switch_a(b, None if first else g0)
                    if tail and j == 2:
                        switch_b(b + 1, 3 * (g0 + 4))
                    j2 = (j + 2) % 4
                    n2 = g0 + j + 2
                    row = "bottom" if tail and j == 1 else "top" if tail and j == 2 else None
                    cast(n2, Q + (j + 2) // 4, j2, cur if j < 2 else nxt, row, first and not (tail and j >= 2))
                    past = not (first and head and j == 0)
                    if past:
                        mish_gap(g0 + j - 1, (j - 1) % 2)
                    l1 = l1_strip(j, kind, era)
                    if l1:
                        off, k = l1
                        relu(4 * (Q + off) + k, 0, b if head and j == 3 else None)
                    if tail and j == 0:
                        stats_group("x", b + 1)
                    if tail and j == 1:
                        hidden_out(b + 1)
                    if tail and j == 2:
                        bias_out(b + 1)
                    if tail and j == 3:
                        taps_high(b + 1, 1, 1 - par)
                    if not first and head and j == 2:
                        stats_group("1", b - 1)
                    if past:
                        mish_exp(g0 + j - 1)
                    evacuate(n2, j2, 0, row, b + 1)
                    if tail and j == 0:
                        stats_rstd("x", b + 1)
                    if not first and head and j == 2:
                        stats_rstd("1", b - 1)
                    if first and head:
                        sums_x(2 * j, 2 * j + 1, None)
                    if past:
                        mish_square(g0 + j - 1)
                        mish_ln(g0 + j - 1)
                    if tail and j == 2:
                        taps_high(b + 1, 0, 1 - par)
                    if tail and j == 3:
                        taps_high(b + 1, 2, 1 - par)
                    if past:
                        mish_inverse(g0 + j - 1)
                    evacuate(n2, j2, 1, row, b + 1)
                    if l1:
                        relu(4 * (Q + off) + k, 1, None)
                    if not first and head and j == 2:
                        layer1_bias(b - 1)
                    if tail and j == 0:
                        pooled_out(b + 1)
                    if tail and j == 1:
                        kernels_out(b + 1)
                    summed = 2 * j + 1 if first and head else g0 + j + STAT - STRIPS
                    if j == 3:
                        squares_1(g0, 0, cur, 4 * q, summed)
                    elif not head:
                        squares_1(g0 + j - 3, j + 1, prev, 4 * q + j - 3, summed)
                    elif not first and j < 2:
                        squares_1(g0 + j - 3, j + 1, prev, STRIPS + j - 3, summed)
                    sums_x(summed if first and head else (0 if tail else 4 * q + 4) + j, summed + 1,
                           None if first and head and j < 3 else g0 + j - 2)
                    if not first and head and j == 1:
                        squares_1(g0 - 1, 3, prev, STRIPS - 1, summed + 1)
                        moments("1", b - 1, g0)
                    evacuate_side(n2, j2, row)

            def epilogue():
                n = B * STRIPS
                mish_gap(n - 1, 1)
                for m in range(n - STRIPS - 3, n - STRIPS):
                    for t in range(2):
                        relu(m, t, None, spill_bank(m, t))
                    if m == n - STRIPS - 3:
                        mish_exp(n - 1)
                        mish_square(n - 1)
                        mish_ln(n - 1)
                        mish_inverse(n - 1)
                for k in range(n - 3, n):
                    squares_1(k, k % 4, slot(k // 4, 0), k % STRIPS, n + STAT - STRIPS)
                    if k < n - 1:
                        eng.wait_ge(s_b1, k + 1)
                moments("1", B - 1, n)
                stats_group("1", B - 1)
                stats_rstd("1", B - 1)
                layer1_bias(B - 1)
                for s in range(STRIPS):
                    for t in range(2):
                        relu(n - STRIPS + s, t, B if s == 0 and t == 0 else None, last_bank(s, t))

            image_loop(eng, prologue, quad, epilogue)

        @block.tensor
        def _(eng):
            mm = nc.tensor.matmul

            def group_moments(who, i):
                eng.wait_ge(hk[who + "mom"], i + 1)
                mm(psM[:, 0:2], groupm[:], st[who]["agg"][:], start=True, stop=True).then_inc(hk[who + "gps"], 1)

            def pooled_products(i):
                eng.wait_ge(hk["xr"], i + 1)
                for h in range(2):
                    last = mm(psM[:, 2 * h:2 * h + 2], wint[:, h * C:(h + 1) * C], st["x"]["mm"][:],
                              start=True, stop=True)
                last.then_inc(s_pps, 1)

            def hidden(i):
                eng.wait_ge(s_pl, i + 1)
                for h in range(2):
                    for k in range(2):
                        last = mm(psM[:, h:h + 1], w1t[:, k, h * C:(h + 1) * C], pooled[:, k:k + 1],
                                  start=(k == 0), stop=(k == 1))
                last.then_inc(s_hps, 1)

            def kernels(i):
                eng.wait_ge(s_hvl, i + 1)
                for h in range(2):
                    for tap in range(TAPS):
                        o = psM[:, 2 * (h * TAPS + tap):2 * (h * TAPS + tap) + 2]
                        for k in range(2):
                            mm(o, w2p[:, 0, k, tap, h * C:(h + 1) * C], hv[:, k, 0:2], start=(k == 0), stop=False)
                            last = mm(o, w2p[:, 1, k, tap, h * C:(h + 1) * C], hv[:, k, 1:3],
                                      start=False, stop=(k == 1))
                last.then_inc(s_kps, 1)

            def bias_rows(i):
                eng.wait_ge(s_bxr, i + 1)
                eng.wait_ge(s_ksb, i + 1)
                mm(psM[0:64, 0:C], bx[:], ident[:], start=True, stop=True).then_inc(s_tps, 1)

            def spread(i, u):
                eng.wait_ge(s_kk, i + 1)
                if u == 0:
                    eng.wait_ge(s_vst, i + 1)
                else:
                    eng.wait_ge(s_wt, 3 * i + u)
                for v in range(3):
                    tap = 3 * u + v
                    last = mm(psM[:, v * C:(v + 1) * C], kk[:, tap:tap + 1].broadcast_to([C, C]), ident[:],
                              start=True, stop=True)
                last.then_inc(s_kbc, 1)

            def conv(n, j, t, tile, taps, par, done=False):
                r0 = 8 * j + 4 * t
                o = psA[:, j % 2, t * TP:(t + 1) * TP].rearrange("p (r c) -> p r c", c=W)[:, :, SIDE:W]
                v0 = {"first": 0, "mid": 1, "last": 2}[tile]
                if taps[0] == 0:
                    mm(o, vb[:], valid[:, v0:v0 + 4, :], start=True, stop=False)
                for tap in taps:
                    dy, dx = tap // 3, tap % 3
                    wh = wa[:, par, 0, tap * C:(tap + 1) * C]
                    wl = wa[:, par, 1, tap * C:(tap + 1) * C]
                    xhi = hi[:, r0 + dy:r0 + dy + 4, SIDE + dx:dx + W]
                    xlo = lo[:, r0 + dy:r0 + dy + 4, SIDE + dx:dx + W]
                    mm(o, wh, xhi, start=False, stop=False)
                    mm(o, wh, xlo, start=False, stop=False)
                    last = mm(o, wl, xhi, start=False, stop=(tap == TAPS - 1))
                if done:
                    last.then_inc(s_cv, 1)

            def product_b(n, j, t, i, bank=None):
                if t == 0:
                    eng.wait_ge(s_hi, n + 1)
                    eng.wait_ge(s_lo, n + 1)
                if i is not None:
                    eng.wait_ge(s_wbh, i + 1)
                    eng.wait_ge(s_wbl, i + 1)
                o = psB[:] if bank is None else bank
                if bank is None:
                    eng.wait_ge(s_xe, 3 * n + t)
                r0 = 8 * j + 4 * t + 1
                xhi = hi[:, r0:r0 + 4, 1:1 + W]
                xlo = lo[:, r0:r0 + 4, 1:1 + W]
                mm(o, wb[:, 0, C:HID], xhi, start=True, stop=False)
                mm(o, wb[:, 0, C:HID], xlo, start=False, stop=False)
                mm(o, wb[:, 1, C:HID], xhi, start=False, stop=True).then_inc(s_xm, 1)

            def product_side(n, j, at=None):
                if at is None:
                    eng.wait_ge(s_xe, 3 * n + 2)
                o = psB[:, 0:ROWS * (SIDE + 1)] if at is None else at
                xhi = hi[:, 8 * j + 1:8 * j + 9, 1:2 + SIDE]
                xlo = lo[:, 8 * j + 1:8 * j + 9, 1:2 + SIDE]
                mm(o, wb[:, 0, 0:C], xhi, start=True, stop=False)
                mm(o, wb[:, 0, 0:C], xlo, start=False, stop=False)
                mm(o, wb[:, 1, 0:C], xhi, start=False, stop=True).then_inc(s_xm, 1)

            def product_out(n, t):
                if t == 0:
                    eng.wait_ge(s_w, n + 1)
                if not isinstance(n, int) or n + t >= 1:
                    eng.wait_ge(s_x1, 2 * n + t)
                for h in range(2):
                    last = mm(psO[:], woutt[:, h, :], wm[:, h * SP + t * TP:h * SP + (t + 1) * TP],
                              start=(h == 0), stop=(h == 1))
                last.then_inc(s_om, 1)

            def layer1(n, k, base, t, i, ps=None, banks=1):
                if i is not None:
                    eng.wait_ge(s_lpt, i)
                eng.wait_ge(s_re, 2 * n + t + 1 - banks + FREE)
                mm(psL[:] if ps is None else ps, lpt[:], X[:, bass.ds(base + k * SP + t * TP, TP)],
                   start=True, stop=True).then_inc(s_lm, 1)

            def layer1_mean(i):
                eng.wait_ge(hk["1r"], i + 1)
                mm(psM[:, 0:1], lt[:], st["1"]["mm"][:, 1:2], start=True, stop=True).then_inc(s_lps, 1)

            def prologue():
                eng.wait_ge(s_const, 16 * len(consts))
                mm(psM[:, 0:C], ampw, cosm, start=True, stop=True)
                mm(psM[:, C:2 * C], phw, sinm, start=True, stop=True).then_inc(s_i, 1)
                eng.wait_ge(s_j, 1)
                mm(psM[:, 0:C], cosm, m1[:, 0:C], start=True, stop=False)
                mm(psM[:, 0:C], sinm, m1[:, C:2 * C], start=False, stop=True)
                mm(psM[:, C:C + 1], cosm, ampb, start=True, stop=False)
                mm(psM[:, C:C + 1], sinm, nphb, start=False, stop=True).then_inc(s_i, 1)
                eng.wait_ge(s_j, 2)
                group_moments("x", 0)
                pooled_products(0)
                hidden(0)
                for n in range(2):
                    for t in range(2):
                        product_b(n, n, t, 0 if n + t == 0 else None, early_bank(n, t))
                    product_side(n, n, early_side(n))
                eng.wait_ge(s_w2l, 2)
                kernels(0)
                bias_rows(0)
                for u in range(3):
                    spread(0, u)

            def quad(b, q, Q, era, kind, par):
                first = era == 0
                g0 = snap(eng, Q * 4)
                if not first:
                    near = snap(eng, slot(Q, -4))
                    far = snap(eng, slot(Q, -5))
                head, tail = kind == "head", kind == "tail"
                for j in range(4):
                    out_n = g0 + j - 2
                    past = not (first and head and j < 2)
                    l1 = l1_strip(j, kind, era)
                    if past:
                        product_out(out_n, 0)
                    if l1:
                        off, k = l1
                        layer1(4 * (Q + off) + k, k, far if off == -5 else near, 0,
                               b if head and j == 3 else None)
                    if tail and j == 0:
                        group_moments("x", b + 1)
                    if tail and j == 1:
                        hidden(b + 1)
                    if tail and j == 2:
                        bias_rows(b + 1)
                    if tail and j == 3:
                        spread(b + 1, 2)
                    if not first and head and j == 2:
                        group_moments("1", b - 1)
                    if head and j == 0:
                        eng.wait_ge(s_wsh, 3 * (b + 1))
                        eng.wait_ge(s_wsl, 3 * (b + 1))
                        eng.wait_ge(s_vb, b + 1)
                    if past:
                        eng.wait_ge(s_w, g0 + j - 1)
                    eng.wait_ge(s_hi, g0 + j + 2)
                    eng.wait_ge(s_lo, g0 + j + 2)
                    tile = "first" if head and j == 0 else "mid"
                    conv(g0 + j, j, 0, tile, range(3), par)
                    product_b(g0 + j + 2, (j + 2) % 4, 0, b + 1 if tail and j == 2 else None)
                    conv(g0 + j, j, 0, tile, range(3, TAPS), par)
                    if not first and head and j == 2:
                        layer1_mean(b - 1)
                    if tail and j == 1:
                        kernels(b + 1)
                    if tail and j == 2:
                        spread(b + 1, 0)
                    if past:
                        product_out(out_n, 1)
                    product_b(g0 + j + 2, (j + 2) % 4, 1, None)
                    if l1:
                        layer1(4 * (Q + off) + k, k, far if off == -5 else near, 1, None)
                    if tail and j == 0:
                        pooled_products(b + 1)
                    if tail and j == 2:
                        spread(b + 1, 1)
                    tile = "last" if tail and j == 3 else "mid"
                    conv(g0 + j, j, 1, tile, range(6), par)
                    product_side(g0 + j + 2, (j + 2) % 4)
                    conv(g0 + j, j, 1, tile, range(6, TAPS), par, True)

            def epilogue():
                n = B * STRIPS
                for t in range(2):
                    product_out(n - 2, t)
                for m in range(n - STRIPS - 3, n - STRIPS):
                    for t in range(2):
                        own = m == n - STRIPS - 3 and t == 0
                        layer1(m, m % 4, slot(m // 4, 0), t, None, spill_bank(m, t), 1 if own else 3)
                for t in range(2):
                    product_out(n - 1, t)
                group_moments("1", B - 1)
                layer1_mean(B - 1)
                for s in range(STRIPS):
                    for t in range(2):
                        m = n - STRIPS + s
                        layer1(m, s % 4, slot(m // 4, 0), t, B if s == 0 and t == 0 else None, last_bank(s, t), 4)

            image_loop(eng, prologue, quad, epilogue)

        @block.vector
        def _(eng):
            V = nc.vector

            def moments_0():
                agg = st["x"]["agg"]
                eng.wait_ge(s_b0, 2 * STRIPS)
                V.bn_aggr(agg[:], bnx).then_inc(hk["xagg"], 1)
                eng.wait_ge(hk["xagg"], 1)
                V.scalar_tensor_tensor(out=agg[:, 1:2], in0=agg[:, 0:1], scalar=agg[:, 0:1],
                                       in1=agg[:, 1:2], op0=ALU.mult, op1=ALU.add).then_inc(hk["xmom"], 1)

            def tap_matrices(i, u):
                eng.wait_ge(s_wn, i + 1)
                eng.wait_ge(s_kbc, 3 * i + u + 1)
                if not isinstance(i, int) or i > 0 or u > 0:
                    eng.wait_ge(s_wsl, 3 * i + u)
                V.tensor_tensor(wtmp[:].rearrange("p (k o) -> p k o", o=C),
                                psM[:, 0:3 * C].rearrange("p (k o) -> p k o", o=C),
                                wn[:, None, 0:C].broadcast_to([C, 3, C]), ALU.mult).then_inc(s_wt, 1)

            def switch_a(i, done):
                eng.wait_ge(s_kk, i + 1)
                if done is not None:
                    eng.wait_ge(s_tap, done * TAPS)
                    eng.wait_ge(s_st, done * TAPS)
                V.tensor_copy(kb[:], kk[:]).then_inc(s_kb, 1)
                eng.wait_ge(s_kb, i + 1)

            def tap(n, j, k):
                if k == 0:
                    eng.wait_ge(s_xe, 3 * n + 4)
                    if not isinstance(n, int) or n >= 2:
                        eng.wait_ge(s_w, n - 1)
                else:
                    eng.wait_ge(s_tap, n * TAPS + k)
                dy, dx = k // 3, k % 3
                src = xh[:, 8 * j + dy:8 * j + dy + 8, dx:dx + W]
                dst = acc[:, j % 2, :].rearrange("p (r c) -> p r c", c=W)
                if k == 0:
                    V.tensor_scalar(dst, src, kb[:, TAPS:TAPS + 1], None, ALU.mult).then_inc(s_tap, 1)
                else:
                    V.scalar_tensor_tensor(out=dst, in0=src, scalar=kb[:, TAPS + k:TAPS + k + 1], in1=dst,
                                           op0=ALU.mult, op1=ALU.add).then_inc(s_tap, 1)

            def side_tap(n, j, k):
                if k == 0:
                    eng.wait_ge(s_xe, 3 * n + 6)
                    if not isinstance(n, int) or n >= 1:
                        eng.wait_ge(s_st, n * TAPS)
                else:
                    eng.wait_ge(s_st, n * TAPS + k)
                dy, dx = k // 3, k % 3
                src = side[:, 8 * j + dy:8 * j + dy + 8, dx:dx + SIDE]
                if k == 0:
                    V.tensor_scalar(sacc[:], src, kb[:, 0:1], None, ALU.mult).then_inc(s_st, 1)
                    return
                dst = sacc[:]
                if k == TAPS - 1:
                    eng.wait_ge(s_cv, n + 1)
                    dst = psA[:, j % 2, :].rearrange("p (r c) -> p r c", c=W)[:, :, 0:SIDE]
                V.scalar_tensor_tensor(out=dst, in0=src, scalar=kb[:, k:k + 1], in1=sacc[:],
                                       op0=ALU.mult, op1=ALU.add).then_inc(s_st, 1)

            def weigh(n, par, h):
                if h == 0:
                    eng.wait_ge(s_act, 4 * n + 4)
                    if not isinstance(n, int) or n >= 1:
                        eng.wait_ge(s_om, 2 * n)
                y = psA[:, par, :] if h == 0 else acc[:, par, :]
                last = V.scalar_tensor_tensor(out=wm[:, h * SP:(h + 1) * SP], in0=em[:, h * SP:(h + 1) * SP],
                                              scalar=0.5, in1=y, op0=ALU.subtract, op1=ALU.mult)
                if h == 1:
                    last.then_inc(s_w, 1)

            def residual(n, k, base, t, s, i=None):
                eng.wait_ge(s_om, 2 * n + t + 1)
                if i is not None:
                    eng.wait_ge(hk["1mom"], i)
                xs = X[:, bass.ds(base + k * SP + t * TP, TP)]
                V.scalar_tensor_tensor(out=xs, in0=psO[:], scalar=boutp[:, 0:1], in1=xs, op0=ALU.add,
                                       op1=ALU.add, accum_out=sum1[:, bass.ds(2 * s + t, 1)]).then_inc(s_x1, 1)

            def prologue():
                V.memset(hi[:], 0.0).then_inc(s_zero, 1)
                V.memset(lo[:], 0.0).then_inc(s_zero, 1)
                V.memset(xh[:], 0.0).then_inc(s_zero, 1)
                V.memset(zero, 0.0).then_inc(s_zero, 1)
                V.memset(bx[:], 0.0).then_inc(s_zero, 1)
                V.memset(hv[:], 0.0).then_inc(s_zero, 1)
                V.memset(side[:], 0.0).then_inc(s_zero, 1)
                V.memset(ymax[:], YMAX).then_inc(s_zero, 1)
                for c in range(2 * STRIPS):
                    if c % 2 == 0:
                        eng.wait_ge(s_first[c // 2], 16)
                    V.bn_stats(bnx[:, c, :], X[:, c * TP:(c + 1) * TP]).then_inc(s_b0, 1)
                moments_0()
                eng.wait_ge(s_const, 16 * len(consts))
                for k in range(2):
                    eng.wait_ge(s_w2h, k + 1)
                    V.tensor_tensor(w2p[:, 1, k], w2t[:, k], w2p[:, 0, k], ALU.subtract).then_inc(s_w2l, 1)
                for u in range(3):
                    tap_matrices(0, u)

            def quad(b, q, Q, era, kind, par):
                first = era == 0
                g0 = snap(eng, Q * 4)
                cur = snap(eng, slot(Q, 0))
                prev = snap(eng, slot(Q, -1))
                head, tail = kind == "head", kind == "tail"
                for j in range(4):
                    n = g0 + j
                    s1 = j - 2 + (STRIPS if head and j < 2 else q * 4)
                    base1 = cur if j >= 2 else prev
                    k1 = (j - 2) % 4
                    out_on = not (first and head and j < 2)
                    mish_on = not (first and head and j == 0)

                    def late(t):
                        if out_on:
                            fresh = head and j == 2 and t == 0 and not first
                            residual(n - 2, k1, base1, t, s1, b if fresh else None)

                    if mish_on:
                        side_tap(n - 1, (j - 1) % 4, TAPS - 1)
                    if head and j == 0:
                        switch_a(b, None if first else g0)
                    tap(n, j, 0)
                    side_tap(n, j, 0)
                    tap(n, j, 1)
                    late(0)
                    for k in range(1, 6):
                        side_tap(n, j, k)
                        tap(n, j, k + 1)
                        if tail and j == 2 and k == 4:
                            tap_matrices(b + 1, 0)
                        if tail and j == 3 and k == 4:
                            tap_matrices(b + 1, 2)
                    side_tap(n, j, 6)
                    tap(n, j, 7)
                    side_tap(n, j, 7)
                    if mish_on:
                        weigh(n - 1, (j - 1) % 2, 0)
                    tap(n, j, 8)
                    if mish_on:
                        weigh(n - 1, (j - 1) % 2, 1)
                    late(1)
                    if tail and j == 2:
                        tap_matrices(b + 1, 1)

            def epilogue():
                n = B * STRIPS
                side_tap(n - 1, 3, TAPS - 1)
                for t in range(2):
                    residual(n - 2, 2, slot((n - 2) // 4, 0), t, STRIPS - 2)
                weigh(n - 1, 1, 0)
                weigh(n - 1, 1, 1)
                for t in range(2):
                    residual(n - 1, 3, slot((n - 1) // 4, 0), t, STRIPS - 1)
                for m in range(n - STRIPS, n):
                    for t in range(2):
                        eng.wait_ge(s_re, 2 * m + t + 1 + FREE)
                        at = slot(m // 4, 0) + (m % 4) * SP + t * TP
                        V.tensor_tensor(X[:, at:at + TP], X[:, at:at + TP], zt[:, t, :], ALU.add).then_inc(s_add, 1)

            image_loop(eng, prologue, quad, epilogue)

        @block.gpsimd
        def _(eng):
            P = nc.gpsimd
            def variance(who, i, s):
                d = st[who]
                eng.wait_ge(hk[who + "gsb"], i + 1)
                P.tensor_tensor(d["t"][:], d["gm"][:, 0:1], d["gm"][:, 0:1], ALU.mult).then_inc(s, 1)
                eng.wait_ge(s, 7 * i + 1)
                P.tensor_tensor(d["t"][:], d["gm"][:, 1:2], d["t"][:], ALU.subtract).then_inc(s, 1)
                eng.wait_ge(s, 7 * i + 2)
                apart(eng)
                P.tensor_scalar(d["v"][:], d["t"][:], EPS, None, ALU.add).then_inc(hk[who + "var"], 1)

            def rstd(who, i, s):
                d = st[who]
                eng.wait_ge(hk[who + "r0"], i + 1)
                P.tensor_tensor(d["t"][:], d["r0"][:], d["r0"][:], ALU.mult).then_inc(s, 1)
                eng.wait_ge(s, 7 * i + 3)
                P.tensor_tensor(d["t"][:], d["t"][:], d["v"][:], ALU.mult).then_inc(s, 1)
                eng.wait_ge(s, 7 * i + 4)
                apart(eng)
                P.tensor_scalar(d["t"][:], d["t"][:], -0.5, 1.5, ALU.mult, ALU.add).then_inc(s, 1)
                eng.wait_ge(s, 7 * i + 5)
                P.tensor_tensor(d["r"][:], d["r0"][:], d["t"][:], ALU.mult).then_inc(s, 1)
                P.tensor_tensor(d["mm"][:, 0:1], d["agg"][:, 0:1], d["gm"][:, 0:1], ALU.subtract).then_inc(hk[who + "pool"], 1)
                eng.wait_ge(s, 7 * i + 6)
                eng.wait_ge(hk[who + "pool"], i + 1 + (who == "1"))
                P.tensor_tensor(d["mm"][:, 0:1], d["mm"][:, 0:1], d["r"][:], ALU.mult).then_inc(s, 1)
                P.tensor_tensor(d["mm"][:, 1:2], d["gm"][:, 0:1], d["r"][:], ALU.mult).then_inc(hk[who + "r"], 1)
                eng.wait_ge(s, 7 * i + 7)
                eng.wait_ge(hk[who + "r"], i + 1)

            def fold(i):
                if not isinstance(i, int) or i > 0:
                    eng.wait_ge(s_wt, 3 * i)
                apart(eng)
                P.tensor_scalar(wn[:], wint[:], st["x"]["r"][:, 0:1], None, ALU.mult).then_inc(s_wn, 1)

            def pool_bias(i):
                pv = pm[:].rearrange("p (h a) -> p a h", a=2)
                eng.wait_ge(s_psb, i + 1)
                P.tensor_tensor(pooled[:], pv[:, 0, :], binp[:], ALU.add)
                P.tensor_tensor(bp[:], binp[:], pv[:, 1, :], ALU.subtract).then_inc(s_pl, 1)

            def hidden_low(i):
                eng.wait_ge(s_hvh, i + 1)
                P.tensor_tensor(hv[:, :, 0], hcx[:], hv[:, :, 1], ALU.subtract).then_inc(s_hvl, 1)

            def kernel_bias(i):
                eng.wait_ge(s_ksb, i + 1)
                kv = kraw[:].rearrange("p (k a) -> p a k", a=2)
                P.tensor_tensor(kk[:], kv[:, 0, :], kv[:, 1, :], ALU.add).then_inc(s_ks, 1)
                eng.wait_ge(s_ks, i + 1)
                P.tensor_tensor(kk[:], kk[:], b2p[:], ALU.add).then_inc(s_kk, 1)
                eng.wait_ge(s_kk, i + 1)
                eng.wait_ge(s_pl, i + 1)
                apart(eng)
                P.tensor_scalar(bk[:], kk[:, 0:TAPS], bp[:, 0:1], None, ALU.mult).then_inc(s_bst, 1)
                eng.wait_ge(s_bst, 2 * i + 1)
                apart(eng)
                P.tensor_copy(bh[:], bk[:]).then_inc(s_bst, 1)
                eng.wait_ge(s_bst, 2 * i + 2)
                apart(eng)
                P.tensor_copy(bx[:, 0:TAPS], bh[:])
                P.tensor_tensor(bx[:, 32:32 + TAPS], bk[:], bh[:], ALU.subtract).then_inc(s_bxr, 1)

            def taps_low(i, u, par):
                eng.wait_ge(s_wsh, 3 * i + u + 1)
                part = slice(3 * u * C, 3 * (u + 1) * C)
                P.tensor_tensor(wa[:, par, 1, part], wtmp[:], wa[:, par, 0, part], ALU.subtract).then_inc(s_wsl, 1)

            def switch_b(i):
                eng.wait_ge(s_wbh, i + 1)
                eng.wait_ge(s_wn, i + 1)
                P.tensor_tensor(wb[:, 1, :], wn[:], wb[:, 0, :], ALU.subtract).then_inc(s_wbl, 1)

            def fold_1(i, done):
                eng.wait_ge(s_re, done)
                apart(eng)
                P.tensor_scalar(lpt[:], lt[:], st["1"]["r"][:, 0:1], None, ALU.mult).then_inc(s_lpt, 1)

            def cast(n, j, base, row):
                eng.wait_ge(s_hi, n + 1)
                xs = X[:, bass.ds(base + j * SP, SP)].rearrange("p (r c) -> p r c", c=W)
                apart(eng)
                if row == "top":
                    P.memset(lo[:, 0, :], 0.0)
                elif row == "bottom":
                    P.memset(lo[:, RING + 1, :], 0.0)
                elif j in (0, 3):
                    p, r = (RING + 1, 0) if j == 0 else (0, ROWS - 1)
                    P.tensor_tensor(lo[:, p, 1:1 + W], xs[:, r, :], hi[:, p, 1:1 + W], ALU.subtract)
                P.tensor_tensor(lo[:, 8 * j + 1:8 * j + 9, 1:1 + W], xs,
                                hi[:, 8 * j + 1:8 * j + 9, 1:1 + W], ALU.subtract).then_inc(s_lo, 1)

            def add(n, k, base, t):
                eng.wait_ge(s_re, 2 * n + t + 1 + FREE)
                xs = X[:, bass.ds(base + k * SP + t * TP, TP)]
                P.tensor_tensor(xs, xs, zt[:, t, :], ALU.add).then_inc(s_add, 1)

            s_px, s_p1 = s_chain["x"], s_chain["1"]

            def prologue():
                eng.wait_ge(s_const, 16 * len(consts))
                eng.wait_ge(s_zero, 8)
                for t in range(FREE):
                    P.memset(bk[:], 0.0).then_inc(s_add, 1)
                    eng.wait_ge(s_add, t + 1)
                P.memset(bk[:], 0.0).then_inc(hk["1pool"], 1)
                eng.wait_ge(hk["1pool"], 1)
                for n in range(2):
                    cast(n, n, 0, "top" if n == 0 else None)
                variance("x", 0, s_px)
                rstd("x", 0, s_px)
                fold(0)
                pool_bias(0)
                switch_b(0)
                hidden_low(0)
                kernel_bias(0)
                for u in range(3):
                    taps_low(0, u, 0)

            def quad(b, q, Q, era, kind, par):
                g0 = snap(eng, Q * 4)
                cur = snap(eng, slot(Q, 0))
                nxt = snap(eng, slot(Q, 1))
                near = snap(eng, slot(Q, -4))
                first = era == 0
                head, tail = kind == "head", kind == "tail"
                for j in range(4):
                    row = "bottom" if tail and j == 1 else "top" if tail and j == 2 else None
                    cast(g0 + j + 2, (j + 2) % 4, cur if j < 2 else nxt, row)
                    if tail and j == 1:
                        hidden_low(b + 1)
                    if tail and j == 2:
                        switch_b(b + 1)
                    if tail and j == 0:
                        variance("x", b + 1, s_px)
                        rstd("x", b + 1, s_px)
                        fold(b + 1)
                    if not first and head and j == 2:
                        variance("1", b - 1, s_p1)
                        rstd("1", b - 1, s_p1)
                    if tail and j == 3:
                        taps_low(b + 1, 1, 1 - par)
                    l1 = l1_strip(j, kind, era)
                    for t in range(2):
                        if l1:
                            off, k = l1
                            add(4 * (Q + off) + k, k, nxt if off == -5 else near, t)
                        if tail and j == 2 and t == 0:
                            taps_low(b + 1, 0, 1 - par)
                        if tail and j == 3 and t == 0:
                            taps_low(b + 1, 2, 1 - par)
                    if not first and head and j == 2:
                        fold_1(b - 1, 2 * (g0 - STRIPS) + FREE)
                    if tail and j == 0:
                        pool_bias(b + 1)
                    if tail and j == 1:
                        kernel_bias(b + 1)

            def epilogue():
                n = B * STRIPS
                for m in range(n - STRIPS - 3, n - STRIPS):
                    for t in range(2):
                        add(m, m % 4, slot(m // 4, 0), t)
                variance("1", B - 1, s_p1)
                rstd("1", B - 1, s_p1)
                fold_1(B - 1, 2 * (n - STRIPS) + FREE)

            image_loop(eng, prologue, quad, epilogue)


def _layout(inputs):
    import numpy as np
    n = lambda k: np.asarray(inputs[k])
    halves = lambda v: np.ascontiguousarray(v.reshape(2, C).T)
    k_in = lambda m: np.ascontiguousarray(m.reshape(2, C, -1).transpose(1, 0, 2))
    a = {}
    a["x"] = n("x").reshape(B, C, H * W)
    a["w_in_t"] = np.ascontiguousarray(n("L0_conv_w_in").T)
    a["b_in"] = halves(n("L0_conv_b_in"))
    a["w1_t"] = k_in(n("L0_conv_kg_w1").T)
    a["b1"] = halves(n("L0_conv_kg_b1"))
    w2 = n("L0_conv_kg_w2").reshape(HID, TAPS, HID).transpose(2, 1, 0)
    a["w2_t"] = np.ascontiguousarray(w2.reshape(2, C, TAPS, HID).transpose(1, 0, 2, 3))
    a["b2"] = np.ascontiguousarray(n("L0_conv_kg_b2").reshape(2, C, TAPS).transpose(1, 0, 2).reshape(C, 2 * TAPS))
    a["w_out_t"] = k_in(n("L0_conv_w_out").T)
    a["b_out"] = n("L0_conv_b_out").reshape(C, 1)
    a["mask"] = n("L1_conv_freq_mask").reshape(C, 1)
    a["amp_w"] = n("L1_conv_amp_w")
    a["amp_b"] = n("L1_conv_amp_b").reshape(C, 1)
    a["ph_w"] = n("L1_conv_phase_w")
    a["ph_b"] = n("L1_conv_phase_b").reshape(C, 1)
    f = (np.arange(C) + C // 2) % C
    angle = 2 * np.pi * (f[:, None] * np.arange(C)[None, :] % C) / C
    a["cos_m"] = np.cos(angle).astype(np.float32)
    a["sin_m"] = np.sin(angle).astype(np.float32)
    g = np.arange(C) // GROUP
    a["group_m"] = ((g[:, None] == g[None, :]) / GROUP).astype(np.float32)
    a["ident_m"] = np.eye(C, dtype=np.float32)
    v = np.zeros((64, 6, W), np.float16)
    for tap in range(TAPS):
        dy, dx = tap // 3, tap % 3
        m = np.ones((6, W))
        if dy == 0:
            m[0] = 0
        if dy == 2:
            m[5] = 0
        if dx == 0:
            m[:, 0] = 0
        if dx == 2:
            m[:, W - 1] = 0
        v[tap] = v[32 + tap] = m
    a["valid_m"] = np.ascontiguousarray(v[:, :, SIDE:])
    return a


def kernel(**inputs):
    import numpy as _np
    import concourse.bacc as _bacc
    from concourse.bass_utils import run_bass_kernel_spmd as _run

    nc = _bacc.Bacc("TRN2", target_bir_lowering=False, num_devices=1)
    arrays, args = {}, {}
    for name, a in _layout(inputs).items():
        arrays[f"in_{name}_dram"] = a
        args[name] = nc.dram_tensor(f"in_{name}_dram", a.shape, mybir.dt.from_np(a.dtype), kind="ExternalInput").ap()
    out = nc.dram_tensor("out_0_dram", (B, C, H * W), F32, kind="ExternalOutput").ap()
    conv_preact_kernel(nc, out=out, **args)
    r = _run(nc, [arrays], core_ids=[0])
    return r.results[0]["out_0_dram"].reshape(B, C, H, W)
```
